# Optimizing a Trainium2 kernel written in Bass

```python
import numpy as np
import jax
import jax.numpy as jnp

def _softmax(x, axis=-1):
    return jax.nn.softmax(x, axis=axis)

def _gelu(x):
    return jax.nn.gelu(x, approximate=True)

def _silu(x):
    return jax.nn.silu(x)

def _sigmoid(x):
    return jax.nn.sigmoid(x)

def _layernorm(x, axis=-1, eps=1e-05):
    m = jnp.mean(x, axis=axis, keepdims=True)
    v = jnp.var(x, axis=axis, keepdims=True)
    return (x - m) / jnp.sqrt(v + eps)

def _scatter_add(tgt, idx, src, axis=0):
    return tgt.at[idx].add(src)

def _segment_sum(src, seg, n):
    return jax.ops.segment_sum(src, seg, n)
kernel_name = 'mk_prb_d2_jaxref_r8_5363b2'

def setup_inputs(seed: int=0):
    np.random.seed(seed)
    _w = jnp.asarray

    def _L0_attn_setup():
        import jax, jax.numpy as jnp
        import numpy as np
        B, N, E = (2, 256, 256)
        H, D = (16, 128)
        BASE = 10000.0

        def rope(t, offset=0):
            d = t.shape[-1]
            pos = jnp.arange(t.shape[1], dtype=jnp.float32) + offset
            inv = BASE ** (-jnp.arange(0, d, 2, dtype=jnp.float32) / d)
            ang = pos[:, None] * inv[None, :]
            cos = jnp.cos(ang)[None, :, None, :]
            sin = jnp.sin(ang)[None, :, None, :]
            t1, t2 = (t[..., :d // 2], t[..., d // 2:])
            return jnp.concatenate([t1 * cos - t2 * sin, t2 * cos + t1 * sin], axis=-1)
        key = jax.random.key(seed)
        ks = jax.random.split(key, 6)
        s = lambda k, shape, fan: jax.random.normal(k, shape, jnp.float32) / np.sqrt(fan)
        return {'x': jax.random.normal(ks[0], (B, N, E), jnp.float32), 'Wq': s(ks[1], (H * D, E), E), 'Wkv': s(ks[2], (2 * D, E), E), 'Wkvh': s(ks[3], (2 * H, E), E), 'Wg': s(ks[4], (2 * H, E), E), 'Wout': s(ks[5], (E, H * D), H * D)}
    _L0_attn_in = _L0_attn_setup()

    def _L0_ffn_setup():
        import jax, jax.numpy as jnp
        import numpy as np
        NUM_EXPERTS = 32
        TOP_K = 4
        HIDDEN = 256
        INTER = 96
        key = jax.random.key(seed)
        k1, k2, k3, k4 = jax.random.split(key, 4)
        hidden_states = jax.random.normal(k1, (4, 64, HIDDEN), dtype=jnp.float32)
        gate = jax.random.normal(k2, (HIDDEN, NUM_EXPERTS), dtype=jnp.float32) * 0.02
        gate_up_proj = jax.random.normal(k3, (NUM_EXPERTS, HIDDEN, 2 * INTER), dtype=jnp.float32) * 0.02
        down_proj = jax.random.normal(k4, (NUM_EXPERTS, INTER, HIDDEN), dtype=jnp.float32) * 0.02
        return {'hidden_states': hidden_states, 'gate': gate, 'gate_up_proj': gate_up_proj, 'down_proj': down_proj}
    _L0_ffn_in = _L0_ffn_setup()

    def _L1_attn_setup():
        import jax, jax.numpy as jnp
        import numpy as np
        N_Q, N_KV = (16, 4)

        def _rope(x):
            d = x.shape[-1]
            T = x.shape[-2]
            inv_freq = 1.0 / 10000.0 ** (jnp.arange(d // 2, dtype=jnp.float32) * 2.0 / d)
            emb = jnp.arange(T, dtype=jnp.float32)[:, None] * inv_freq[None, :]
            cos, sin = (jnp.cos(emb), jnp.sin(emb))
            x1, x2 = (x[..., 0::2], x[..., 1::2])
            return jnp.concatenate([x1 * cos - x2 * sin, x1 * sin + x2 * cos], axis=-1)
        key = jax.random.key(seed)
        ks = jax.random.split(key, 5)
        B, T, C = (4, 256, 256)
        g = N_Q // N_KV
        Ckv = C // g
        s = 0.02
        return {'x': jax.random.normal(ks[0], (B, T, C), dtype=jnp.float32), 'Wq': jax.random.normal(ks[1], (C, C), dtype=jnp.float32) * s, 'bq': jnp.zeros((C,), dtype=jnp.float32), 'Wk': jax.random.normal(ks[2], (C, Ckv), dtype=jnp.float32) * s, 'bk': jnp.zeros((Ckv,), dtype=jnp.float32), 'Wv': jax.random.normal(ks[3], (C, Ckv), dtype=jnp.float32) * s, 'bv': jnp.zeros((Ckv,), dtype=jnp.float32), 'Wo': jax.random.normal(ks[4], (Ckv, C), dtype=jnp.float32) * s, 'bo': jnp.zeros((C,), dtype=jnp.float32)}
    _L1_attn_in = _L1_attn_setup()

    def _L1_ffn_setup():
        import jax, jax.numpy as jnp
        import numpy as np
        H = 256
        I = 128
        E = 32
        K = 4
        N_SHARED = 1
        EPS = 1e-06

        def _rmsnorm(x, w, eps=EPS):
            var = jnp.mean(jnp.square(x), axis=-1, keepdims=True)
            return x * jax.lax.rsqrt(var + eps) * w

        def _moe_core(x, gate_w, w13, w2):
            T = x.shape[0]
            N = T * K
            C = 2 * N // E
            logits = jnp.einsum('th,eh->te', x.astype(jnp.float32), gate_w.astype(jnp.float32))
            scores = jax.nn.softmax(logits, axis=-1)
            topk_w, topk_ids = jax.lax.top_k(scores, K)
            topk_w = topk_w / jnp.sum(topk_w, axis=-1, keepdims=True)
            flat_ids = topk_ids.reshape(-1)
            flat_w = topk_w.reshape(-1)
            order = jnp.argsort(flat_ids)
            sorted_eid = flat_ids[order]
            tok = order // K
            counts = jnp.zeros((E,), jnp.int32).at[flat_ids].add(1)
            starts = jnp.cumsum(counts) - counts
            pos = jnp.arange(N) - starts[sorted_eid]
            buf = jnp.zeros((E, C, x.shape[1]), x.dtype).at[sorted_eid, pos].set(x[tok], mode='drop')
            gu = jnp.einsum('ech,ehf->ecf', buf, w13)
            g, u = jnp.split(gu, 2, axis=-1)
            act = jax.nn.silu(g) * u
            eo = jnp.einsum('eci,eih->ech', act, w2)
            out_slots = eo[sorted_eid, pos]
            routed = jnp.zeros_like(x).at[tok].add(out_slots * flat_w[order][:, None])
            return routed
        key = jax.random.key(seed)
        ks = jax.random.split(key, 8)
        s = 1.0 / np.sqrt(H)
        si = 1.0 / np.sqrt(I)
        return {'hidden_states': jax.random.normal(ks[0], (1, 512, H), jnp.float32), 'norm_w': jnp.ones((H,), jnp.float32), 'gate_w': jax.random.normal(ks[1], (E, H), jnp.float32) * s, 'w13': jax.random.normal(ks[2], (E, H, 2 * I), jnp.float32) * s, 'w2': jax.random.normal(ks[3], (E, I, H), jnp.float32) * si, 'shared_gate_w': jax.random.normal(ks[4], (H, I * N_SHARED), jnp.float32) * s, 'shared_up_w': jax.random.normal(ks[5], (H, I * N_SHARED), jnp.float32) * s, 'shared_down_w': jax.random.normal(ks[6], (I * N_SHARED, H), jnp.float32) * si}
    _L1_ffn_in = _L1_ffn_setup()
    _d = {'L0_attn_x': _L0_attn_in['x'], 'L0_attn_Wq': _L0_attn_in['Wq'], 'L0_attn_Wkv': _L0_attn_in['Wkv'], 'L0_attn_Wkvh': _L0_attn_in['Wkvh'], 'L0_attn_Wg': _L0_attn_in['Wg'], 'L0_attn_Wout': _L0_attn_in['Wout'], 'L0_ffn_gate': _L0_ffn_in['gate'], 'L0_ffn_gate_up_proj': _L0_ffn_in['gate_up_proj'], 'L0_ffn_down_proj': _L0_ffn_in['down_proj'], 'L1_attn_Wq': _L1_attn_in['Wq'], 'L1_attn_bq': _L1_attn_in['bq'], 'L1_attn_Wk': _L1_attn_in['Wk'], 'L1_attn_bk': _L1_attn_in['bk'], 'L1_attn_Wv': _L1_attn_in['Wv'], 'L1_attn_bv': _L1_attn_in['bv'], 'L1_attn_Wo': _L1_attn_in['Wo'], 'L1_attn_bo': _L1_attn_in['bo'], 'L1_ffn_norm_w': _L1_ffn_in['norm_w'], 'L1_ffn_gate_w': _L1_ffn_in['gate_w'], 'L1_ffn_w13': _L1_ffn_in['w13'], 'L1_ffn_w2': _L1_ffn_in['w2'], 'L1_ffn_shared_gate_w': _L1_ffn_in['shared_gate_w'], 'L1_ffn_shared_up_w': _L1_ffn_in['shared_up_w'], 'L1_ffn_shared_down_w': _L1_ffn_in['shared_down_w']}
    _x0 = _d['L0_attn_x']
    _d['L0_attn_x'] = jax.random.normal(jax.random.fold_in(jax.random.key(seed), 1), (4, 512, 256), dtype=_x0.dtype)
    del _x0
    return _d

def reference(L0_attn_x, L0_attn_Wq, L0_attn_Wkv, L0_attn_Wkvh, L0_attn_Wg, L0_attn_Wout, L0_ffn_gate, L0_ffn_gate_up_proj, L0_ffn_down_proj, L1_attn_Wq, L1_attn_bq, L1_attn_Wk, L1_attn_bk, L1_attn_Wv, L1_attn_bv, L1_attn_Wo, L1_attn_bo, L1_ffn_norm_w, L1_ffn_gate_w, L1_ffn_w13, L1_ffn_w2, L1_ffn_shared_gate_w, L1_ffn_shared_up_w, L1_ffn_shared_down_w):

    def _L0_attn_ref(x, Wq, Wkv, Wkvh, Wg, Wout):
        import jax, jax.numpy as jnp
        import numpy as np
        B, N, E = (2, 256, 256)
        H, D = (16, 128)
        BASE = 10000.0

        def rope(t, offset=0):
            d = t.shape[-1]
            pos = jnp.arange(t.shape[1], dtype=jnp.float32) + offset
            inv = BASE ** (-jnp.arange(0, d, 2, dtype=jnp.float32) / d)
            ang = pos[:, None] * inv[None, :]
            cos = jnp.cos(ang)[None, :, None, :]
            sin = jnp.sin(ang)[None, :, None, :]
            t1, t2 = (t[..., :d // 2], t[..., d // 2:])
            return jnp.concatenate([t1 * cos - t2 * sin, t2 * cos + t1 * sin], axis=-1)
        b, n, _ = x.shape
        q = (x @ Wq.T).reshape(b, n, H, D)
        kv = x @ Wkv.T
        kv_head = x @ Wkvh.T
        g = x @ Wg.T
        log_f = jnp.concatenate([jnp.zeros((b, 1, 2 * H), jnp.float32), jax.nn.log_sigmoid(g)], axis=1)
        log_f_cumsum = jnp.cumsum(log_f, axis=1)[:, :-1]
        kv_head = kv_head * jnp.exp(log_f_cumsum)
        kv_head = jnp.cumsum(kv_head, axis=1)
        kp, vp = (kv[..., :D], kv[..., D:])
        kh, vh = (kv_head[..., :H], kv_head[..., H:])
        k = jnp.einsum('bnd,bnh->bnhd', kp, kh)
        v = jnp.einsum('bnd,bnh->bnhd', vp, vh)
        q = rope(q)
        k = rope(k)
        scale = 1.0 / np.sqrt(D)
        scores = jnp.einsum('bnhd,bmhd->bhnm', q, k) * scale
        mask = jnp.tril(jnp.ones((n, n), bool))
        scores = jnp.where(mask[None, None], scores, -jnp.inf)
        p = jax.nn.softmax(scores, axis=-1)
        o = jnp.einsum('bhnm,bmhd->bnhd', p, v).reshape(b, n, H * D)
        return o @ Wout.T

    def _L0_ffn_ref(hidden_states, gate, gate_up_proj, down_proj):
        import jax, jax.numpy as jnp
        import numpy as np
        NUM_EXPERTS = 32
        TOP_K = 4
        HIDDEN = 256
        INTER = 96
        batch_size = hidden_states.shape[0]
        x = hidden_states.reshape(-1, HIDDEN)
        num_tokens = x.shape[0]
        router_logits = jnp.einsum('TD,DE->TE', x, gate)
        routing_weights = jax.nn.softmax(router_logits.astype(jnp.float32), axis=-1)
        top_k_weights, top_k_indices = jax.lax.top_k(routing_weights, TOP_K)
        top_k_weights = top_k_weights / top_k_weights.sum(axis=-1, keepdims=True)
        top_k_weights = top_k_weights.astype(x.dtype)
        router_weights = jnp.zeros((num_tokens, NUM_EXPERTS), dtype=x.dtype)
        token_indices = jnp.broadcast_to(jnp.arange(num_tokens)[:, None], top_k_indices.shape)
        router_weights = router_weights.at[token_indices, top_k_indices].set(top_k_weights)
        gate_up = jnp.einsum('TD,EDF->TEF', x, gate_up_proj)
        g, u = jnp.split(gate_up, 2, axis=-1)
        gated = u * jax.nn.silu(g)
        next_states = jnp.einsum('TEF,EFD->TED', gated, down_proj)
        next_states = (next_states * router_weights[..., None]).sum(axis=1)
        return next_states.reshape(batch_size, -1, HIDDEN)

    def _L1_attn_ref(x, Wq, bq, Wk, bk, Wv, bv, Wo, bo):
        import jax, jax.numpy as jnp
        import numpy as np
        N_Q, N_KV = (16, 4)

        def _rope(x):
            d = x.shape[-1]
            T = x.shape[-2]
            inv_freq = 1.0 / 10000.0 ** (jnp.arange(d // 2, dtype=jnp.float32) * 2.0 / d)
            emb = jnp.arange(T, dtype=jnp.float32)[:, None] * inv_freq[None, :]
            cos, sin = (jnp.cos(emb), jnp.sin(emb))
            x1, x2 = (x[..., 0::2], x[..., 1::2])
            return jnp.concatenate([x1 * cos - x2 * sin, x1 * sin + x2 * cos], axis=-1)
        B, T, C = x.shape
        g = N_Q // N_KV
        d = C // N_Q
        q = (x @ Wq + bq).reshape(B, T, N_Q, d).transpose(0, 2, 1, 3)
        k = (x @ Wk + bk).reshape(B, T, N_KV, d).transpose(0, 2, 1, 3)
        v = (x @ Wv + bv).reshape(B, T, N_KV, d).transpose(0, 2, 1, 3)
        q = _rope(q)
        k = _rope(k)
        qg = q.reshape(B, N_KV, g, T, d)
        scores = jnp.einsum('bhgnd,bhsd->bhns', qg, k) * (1.0 / jnp.sqrt(jnp.float32(d)))
        mask = jnp.tril(jnp.ones((T, T), dtype=bool))
        att = jax.nn.softmax(jnp.where(mask, scores, -jnp.inf), axis=-1)
        y = jnp.einsum('bhns,bhsd->bhnd', att, v)
        y = y.transpose(0, 2, 1, 3).reshape(B, T, C // g)
        return y @ Wo + bo

    def _L1_ffn_ref(hidden_states, norm_w, gate_w, w13, w2, shared_gate_w, shared_up_w, shared_down_w):
        import jax, jax.numpy as jnp
        import numpy as np
        H = 256
        I = 128
        E = 32
        K = 4
        N_SHARED = 1
        EPS = 1e-06

        def _rmsnorm(x, w, eps=EPS):
            var = jnp.mean(jnp.square(x), axis=-1, keepdims=True)
            return x * jax.lax.rsqrt(var + eps) * w

        def _moe_core(x, gate_w, w13, w2):
            T = x.shape[0]
            N = T * K
            C = 2 * N // E
            logits = jnp.einsum('th,eh->te', x.astype(jnp.float32), gate_w.astype(jnp.float32))
            scores = jax.nn.softmax(logits, axis=-1)
            topk_w, topk_ids = jax.lax.top_k(scores, K)
            topk_w = topk_w / jnp.sum(topk_w, axis=-1, keepdims=True)
            flat_ids = topk_ids.reshape(-1)
            flat_w = topk_w.reshape(-1)
            order = jnp.argsort(flat_ids)
            sorted_eid = flat_ids[order]
            tok = order // K
            counts = jnp.zeros((E,), jnp.int32).at[flat_ids].add(1)
            starts = jnp.cumsum(counts) - counts
            pos = jnp.arange(N) - starts[sorted_eid]
            buf = jnp.zeros((E, C, x.shape[1]), x.dtype).at[sorted_eid, pos].set(x[tok], mode='drop')
            gu = jnp.einsum('ech,ehf->ecf', buf, w13)
            g, u = jnp.split(gu, 2, axis=-1)
            act = jax.nn.silu(g) * u
            eo = jnp.einsum('eci,eih->ech', act, w2)
            out_slots = eo[sorted_eid, pos]
            routed = jnp.zeros_like(x).at[tok].add(out_slots * flat_w[order][:, None])
            return routed
        B, S, Hd = hidden_states.shape
        residual = hidden_states
        h = _rmsnorm(hidden_states, norm_w)
        x = h.reshape(-1, Hd)
        routed = _moe_core(x, gate_w, w13, w2)
        shared = jax.nn.silu(x @ shared_gate_w) * (x @ shared_up_w) @ shared_down_w
        out = residual + (routed + shared).reshape(B, S, Hd)
        return out
    x = L0_attn_x
    xn = _layernorm(x, axis=-1)
    x = x + _L0_attn_ref(xn, L0_attn_Wq, L0_attn_Wkv, L0_attn_Wkvh, L0_attn_Wg, L0_attn_Wout) + _L0_ffn_ref(xn, L0_ffn_gate, L0_ffn_gate_up_proj, L0_ffn_down_proj)
    xn = _layernorm(x, axis=-1)
    x = x + _L1_attn_ref(xn, L1_attn_Wq, L1_attn_bq, L1_attn_Wk, L1_attn_bk, L1_attn_Wv, L1_attn_bv, L1_attn_Wo, L1_attn_bo) + _L1_ffn_ref(xn, L1_ffn_norm_w, L1_ffn_gate_w, L1_ffn_w13, L1_ffn_w2, L1_ffn_shared_gate_w, L1_ffn_shared_up_w, L1_ffn_shared_down_w)
    return x

_drawn_inputs = setup_inputs


def setup_inputs(seed=0):
    import zlib

    import numpy as np

    out = dict(_drawn_inputs(seed))
    spreads = {'L1_attn_bq': (0.0, 0.8),
     'L1_attn_bk': (0.0, 0.8),
     'L1_attn_bv': (0.0, 0.8),
     'L1_attn_bo': (0.0, 0.341),
     'L1_ffn_norm_w': (1.0, 0.2)}
    factors = {'L0_ffn_gate': 6.02,
     'L0_ffn_gate_up_proj': 6.039,
     'L0_ffn_down_proj': 5.464,
     'L1_attn_Wq': 8.0,
     'L1_attn_Wk': 8.0,
     'L1_attn_Wv': 8.0,
     'L1_attn_Wo': 7.103}
    for name, (base, spread) in spreads.items():
        noise = np.random.default_rng([zlib.crc32(name.encode()), seed]).standard_normal(out[name].shape)
        drawn = base * np.exp(spread * noise) if base else spread * noise
        out[name] = jnp.asarray(drawn.astype(out[name].dtype))
    for name, factor in factors.items():
        out[name] = (out[name] * factor).astype(out[name].dtype)
    return out
```

```python
from contextlib import ExitStack, contextmanager

import numpy as np

import concourse.bass as bass
import concourse.mybir as mybir

F32 = mybir.dt.float32
BF16 = mybir.dt.bfloat16
I32 = mybir.dt.int32
U32 = mybir.dt.uint32
ALU = mybir.AluOpType
ACT = mybir.ActivationFunctionType
AX = mybir.AxisListType

P = 128
BATCH, SEQ, EMB = 4, 512, 256
TOKENS = BATCH * SEQ
TILES = TOKENS // P
ROWS = SEQ // P
KC = EMB // P
EXPERTS, TOPK = 32, 4
SLOT_TILES = 96
SLOTS = SLOT_TILES * P
UNROLL = 4
CAP1 = 2 * TOKENS * TOPK // EXPERTS
OUT_OF_RANGE = 1 << 16
H0, D0, I0 = 16, 128, 96
H1, D1, I1 = 4, 16, 128
HP1 = 32
GROUPS1 = 4
MASKED = -1e30

PV0, PKH0, PG0, PGATE0 = 0, D0, D0 + 2 * H0, D0 + 4 * H0
PROJ0 = PGATE0 + EXPERTS
_CONST = dict(ident=P, before=P, upto=P, ones=P, mask=P, iota=EXPERTS, index=1,
              cos0=SEQ, sin0=SEQ)


def const_at(name):
    at = 0
    for n, w in _CONST.items():
        if n == name:
            return at, at + w
        at += w
    raise KeyError(name)


CONST_W = sum(_CONST.values())


class Buffers:
    pass


def make_buffers(nc, ctx):
    s = Buffers()

    def sb(name, shape, dt=F32):
        t = ctx.enter_context(nc.sbuf_tensor(name, shape, dt))
        return t

    s.const = sb("const", [P, CONST_W])
    s.identb = sb("identb", [P, P], BF16)
    s.maskb = sb("maskb", [P, P], BF16)
    s.beforeb = sb("beforeb", [P, P], BF16)
    s.onesb = sb("onesb", [P, P], BF16)
    s.x = sb("x_res", [P, TILES, EMB])
    s.xn = sb("xn", [P, TILES, EMB])
    s.xnT = sb("xnT", [P, KC, TOKENS])
    s.big_a = sb("big_a", [P, 80 * 256])
    s.big_b = sb("big_b", [P, 32 * 256])
    s.probs = sb("probs", [P, 2, 1280])
    s.probsT = sb("probsT", [P, 1280])
    s.qT = sb("qT", [P, 2, SEQ])
    s.kT = sb("kT", [P, 2, SEQ])
    s.khb = sb("khb", [P, 2, SEQ])
    s.wq = sb("wq", [P, 2, KC, P])
    s.rope = sb("rope", [P, 2, SEQ])
    s.rope_a, s.rope_b = s.rope[:, 0], s.rope[:, 1]
    s.kh = sb("kh", [P, TILES, 2 * H0])
    s.weight = sb("weight", [P, TILES, TOPK])
    s.slot_w = sb("slot_w", [P, TOPK, TILES], I32)
    s.slot_r = sb("slot_r", [P, TOPK, TILES], I32)
    s.tile_expert = sb("tile_expert", [1, SLOT_TILES], I32)
    s.logits = sb("logits", [P, TILES, EXPERTS])
    s.negmax = sb("negmax", [P, 2, ROWS])
    s.psumrow = sb("sumrow", [P, 2, ROWS])
    s.rsum = sb("rsum", [P, 2, ROWS])
    s.stats = sb("stats", [P, TILES, 6])
    s.meanvar = sb("meanvar", [P, TILES, 2])
    s.rstd = sb("rstd", [P, TILES])
    s.ps = [ctx.enter_context(nc.psum_tensor(f"bank{i}", [P, 512], F32)) for i in range(8)]

    def const(name):
        a, b = const_at(name)
        return s.const[:, a:b]

    s.c = const
    s.gu0 = s.big_a[:, 0:KC * EXPERTS * 2 * I0].rearrange("p (k n) -> p k n", k=KC)
    s.oT = s.big_a[:, 48 * 256:80 * 256].rearrange("p (h n) -> p h n", h=H0)
    s.dn0 = s.big_a[0:I0, 48 * 256:80 * 256]
    s.wout = s.big_b[:, 0:16 * 256].rearrange("p (h n) -> p h n", h=H0)
    s.kpT = s.big_b[:, 16 * 256:24 * 256]
    s.vp = s.big_b[:, 24 * 256:32 * 256].rearrange("p (t n) -> p t n", t=TILES)
    s.gu1 = s.big_a[:, 0:KC * EXPERTS * 2 * I1].rearrange("p (k n) -> p k n", k=KC)
    s.dn1 = s.big_b[:, :]
    s.gath = [s.big_a[:, at:at + UNROLL * EMB].rearrange("p (j e) -> p j e", j=UNROLL) for at in (0, 64 * 256)]
    return s


@contextmanager
def signals(nc, tag):
    made = []

    def sem(name):
        made.append(nc.alloc_semaphore(name=f"{name}_{tag}"))
        return made[-1]

    yield sem
    nc.clear_and_free_semaphores(made)
    nc.all_engine_barrier()


class Link:

    def __init__(self, eng, sem):
        self.eng, self.sem, self.n = eng, sem, 0

    def __call__(self, ins):
        self.n += 1
        ins.then_inc(self.sem, 1)
        self.eng.wait_ge(self.sem, self.n)




def norm_block0(nc, s, d):
    wcat = s.big_a[:, 0:KC * PROJ0].rearrange("p (k n) -> p k n", k=KC)
    wk = s.big_a[:, 512:512 + KC * P].rearrange("p (k n) -> p k n", k=KC)
    zeros = s.big_a[:, 2048:2048 + 2048]
    kg = s.big_a[:, 4096:4096 + TILES * 4 * H0].rearrange("p (t n) -> p t n", t=TILES)
    with signals(nc, "n0") as sem, ExitStack() as ctx:
        const_in, x_in, w_in, zero_made, xs_zeroed = map(sem, ("const_in", "x_in0", "w_in0", "zero_made", "xs_zeroed"))
        cast, stat, aggr, var_ready, std_ready, rstd_ready, xn_ready = map(
            sem, ("cast", "stat0", "aggr0", "var0", "std0", "rstd0", "xn0"))
        turned, xnT_ready, proj_done, vp_out, kg_out, kp_done, kp_part, kp_ready = map(
            sem, ("turned0", "xnT0", "proj0", "vp_out", "kg_out", "kp_done", "kp_part", "kp_ready"))
        x_ins = [x_in] + [sem(f"x_in0_{i}") for i in range(1, 4)]
        block = ctx.enter_context(nc.Block())

        @block.sync
        def _(sp):
            xv = d["x"].rearrange("(t p) e -> p t e", p=P)
            sp.dma_start(s.x[:, 0:4], xv[:, 0:4]).then_inc(x_ins[0], 16)
            sp.dma_start(s.const[:], d["const"]).then_inc(const_in, 16)
            for c in range(1, 4):
                sp.dma_start(s.x[:, 4 * c:4 * c + 4], xv[:, 4 * c:4 * c + 4]).then_inc(x_ins[c], 16)
            sp.dma_start(wcat, d["wcat0"].rearrange("(k p) n -> p k n", p=P)).then_inc(w_in, 16)
            sp.dma_start(wk, d["wk0"].rearrange("(k p) n -> p k n", p=P)).then_inc(w_in, 16)
            sp.dma_start(s.wout, d["wout0"].rearrange("(h p) n -> p h n", p=P)).then_inc(w_in, 16)
            sp.wait_ge(zero_made, 1)
            xs = d["xs"].rearrange("(p r) e -> p (r e)", p=P)
            for c in range(12):
                sp.dma_start(xs[:, 2048 * c:2048 * (c + 1)], zeros).then_inc(xs_zeroed, 16)
            sp.wait_ge(w_in, 48)
            sp.wait_ge(xs_zeroed, 16 * 12)

        @block.gpsimd
        def _(pool):
            nc.gpsimd.memset(zeros, 0.0).then_inc(zero_made, 1)

        @block.vector
        def _(dve):
            for t in range(TILES):
                dve.wait_ge(x_ins[t // 4], 16)
                nc.vector.bn_stats(s.stats[:, t, :], s.x[:, t, :]).then_inc(stat, 1)
            for t in range(TILES):
                dve.wait_ge(stat, t + 1)
                nc.vector.bn_aggr(s.meanvar[:, t, :], s.stats[:, t, :]).then_inc(aggr, 1)
            dve.wait_ge(aggr, TILES)
            nc.vector.tensor_scalar(s.rstd[:], s.meanvar[:, :, 1], 1e-5, None, ALU.add).then_inc(var_ready, 1)
            dve.wait_ge(const_in, 16)
            nc.vector.tensor_copy(s.identb[:], s.c("ident")).then_inc(cast, 1)
            nc.vector.tensor_copy(s.maskb[:], s.c("mask")).then_inc(cast, 1)
            nc.vector.tensor_copy(s.beforeb[:], s.c("before")).then_inc(cast, 1)
            nc.vector.tensor_copy(s.onesb[:], s.c("ones")).then_inc(cast, 1)
            dve.wait_ge(std_ready, 1)
            nc.vector.reciprocal(s.rstd[:], s.rstd[:]).then_inc(rstd_ready, 1)
            dve.wait_ge(rstd_ready, 1)
            for t in range(TILES):
                nc.vector.tensor_scalar(s.xn[:, t, :], s.x[:, t, :], s.meanvar[:, t, 0:1], s.rstd[:, t:t + 1],
                                        ALU.subtract, ALU.mult).then_inc(xn_ready, 1)
            for g in range(TILES // 2):
                dve.wait_ge(proj_done, 2 * g + 2)
                src = s.ps[4 + g % 4][:, 0:2 * PROJ0].rearrange("p (t n) -> p t n", t=2)
                dve.wait_ge(vp_out, g + 1)
                nc.vector.tensor_copy(kg[:, 2 * g:2 * g + 2, :], src[:, :, PKH0:PGATE0]).then_inc(kg_out, 1)
                nc.vector.tensor_copy(s.logits[:, 2 * g:2 * g + 2, :], src[:, :, PGATE0:PROJ0]).then_inc(kg_out, 1)
            for b in range(BATCH):
                dve.wait_ge(kp_done, b + 1)
                src = s.ps[b]
                dst = s.kpT[:, b * SEQ:(b + 1) * SEQ]
                if b:
                    dve.wait_ge(kp_ready, b)
                rope0(nc, s, src).then_inc(kp_part, 1)
                dve.wait_ge(kp_part, b + 1)
                nc.vector.tensor_tensor(dst, s.rope_a, s.rope_b, ALU.add).then_inc(kp_ready, 1)

        @block.scalar
        def _(act):
            act.wait_ge(var_ready, 1)
            nc.scalar.activation(s.rstd[:], s.rstd[:], ACT.Sqrt).then_inc(std_ready, 1)
            for g in range(TILES // 4 * KC):
                act.wait_ge(turned, g + 1)
                nc.scalar.activation(s.xnT[:, g % KC, g // KC * 512:(g // KC + 1) * 512], s.ps[g % 4][:, :],
                                     ACT.Copy).then_inc(xnT_ready, 1)
            for g in range(TILES // 2):
                act.wait_ge(proj_done, 2 * g + 2)
                src = s.ps[4 + g % 4][:, 0:2 * PROJ0].rearrange("p (t n) -> p t n", t=2)
                nc.scalar.activation(s.vp[:, 2 * g:2 * g + 2, :], src[:, :, PV0:PV0 + D0], ACT.Copy).then_inc(vp_out, 1)

        @block.tensor
        def _(pe):
            pe.wait_ge(const_in, 16)
            for g in range(TILES // 4 * KC):
                c, k = g // KC, g % KC
                pe.wait_ge(xn_ready, 4 * c + 4)
                if g >= 4:
                    pe.wait_ge(xnT_ready, g - 3)
                for i in range(4):
                    mm = nc.tensor.transpose(s.ps[g % 4][:, i * P:(i + 1) * P],
                                             s.xn[:, 4 * c + i, k * P:(k + 1) * P], s.c("ident"))
                mm.then_inc(turned, 1)
            pe.wait_ge(w_in, 48)
            for t in range(TILES):
                pe.wait_ge(xnT_ready, KC * (t // 4) + KC)
                if t % 2 == 0 and t >= 8:
                    pe.wait_ge(kg_out, 2 * (t // 2 - 3))
                at = (t % 2) * PROJ0
                for k in range(KC):
                    mm = nc.tensor.matmul(s.ps[4 + t // 2 % 4][:, at:at + PROJ0], s.xnT[:, k, t * P:(t + 1) * P],
                                          wcat[:, k, :], start=k == 0, stop=k == KC - 1)
                mm.then_inc(proj_done, 1)
            pe.wait_ge(xnT_ready, TILES // 4 * KC)
            for b in range(BATCH):
                for k in range(KC):
                    mm = nc.tensor.matmul(s.ps[b][:, :], wk[:, k, :], s.xnT[:, k, b * SEQ:(b + 1) * SEQ],
                                          start=k == 0, stop=k == KC - 1)
                mm.then_inc(kp_done, 1)


def rope0(nc, s, src):
    h = D0 // 2
    cos, sin = s.c("cos0"), s.c("sin0")
    nc.vector.tensor_tensor(s.rope_a, src[:, :], cos, ALU.mult)
    nc.vector.tensor_tensor(s.rope_b[h:, :], src[0:h, :], sin[0:h, :], ALU.mult)
    return nc.vector.tensor_tensor(s.rope_b[0:h, :], src[h:, :], sin[h:, :], ALU.mult)




def gains_block0(nc, s, d):
    n = TILES * 2 * H0
    kg = s.big_a[:, 4096:4096 + TILES * 4 * H0].rearrange("p (t n) -> p t n", t=TILES)
    proj, gate = kg[:, :, 0:2 * H0], kg[:, :, 2 * H0:4 * H0]
    at = 8192

    def scratch():
        nonlocal at
        at += n
        return s.big_a[:, at - n:at].rearrange("p (t h) -> p t h", t=TILES)

    mag, logf, soft, tot, cum = (scratch() for _ in range(5))
    khT = s.probs[0:H0, :, :].rearrange("p a n -> p (a n)")[:, 0:TOKENS]

    def by_row(a):
        return a.rearrange("p (b i) h -> p b i h", b=BATCH)

    with signals(nc, "g0") as sem, ExitStack() as ctx:
        dlink, alink = sem("gain_dve"), sem("gain_act")
        mag_ready, soft_ready, summed, exp_ready, turned, khT_ready, kh_out = map(
            sem, ("mag", "soft", "summed", "expcum", "khturned", "khT", "kh_out"))
        block = ctx.enter_context(nc.Block())

        @block.scalar
        def _(act):
            link = Link(act, alink)
            act.wait_ge(mag_ready, 1)
            link(nc.scalar.activation(mag, mag, ACT.Exp))
            nc.scalar.activation(soft, mag, ACT.Ln, bias=1.0).then_inc(soft_ready, 1)
            act.wait_ge(dlink, 7)
            nc.scalar.activation(cum, cum, ACT.Exp).then_inc(exp_ready, 1)

        @block.vector
        def _(dve):
            link = Link(dve, dlink)
            nc.vector.scalar_tensor_tensor(out=mag, in0=gate, scalar=-1.0, in1=gate, op0=ALU.mult,
                                           op1=ALU.min).then_inc(mag_ready, 1)
            link(nc.vector.tensor_scalar(logf, gate, 0.0, None, ALU.min))
            dve.wait_ge(soft_ready, 1)
            link(nc.vector.tensor_tensor(logf, logf, soft, ALU.subtract))
            for step in range(2):
                dve.wait_ge(summed, 2 * step + 2)
                link(nc.vector.tensor_copy(tot, s.ps[1][:, :].rearrange("p (t h) -> p t h", t=TILES)))
                for i in range(1, ROWS - 1):
                    link(nc.vector.tensor_tensor(by_row(tot)[:, :, i, :], by_row(tot)[:, :, i, :],
                                                 by_row(tot)[:, :, i - 1, :], ALU.add))
                out = cum if step == 0 else s.kh[:]
                part = s.ps[0][:, :].rearrange("p (t h) -> p t h", t=TILES)
                link(nc.vector.tensor_copy(out, part))
                link(nc.vector.tensor_tensor(by_row(out)[:, :, 1:, :], by_row(out)[:, :, 1:, :],
                                             by_row(tot)[:, :, 0:ROWS - 1, :], ALU.add))
                if step == 0:
                    dve.wait_ge(exp_ready, 1)
                    link(nc.vector.tensor_tensor(logf, proj, cum, ALU.mult))
            for c in range(4):
                dve.wait_ge(turned, c + 1)
                nc.vector.tensor_scalar(khT[:, c * 512:(c + 1) * 512], s.ps[2 + c][0:H0, :], D0 ** -0.5, None,
                                        ALU.mult).then_inc(khT_ready, 1)

        @block.tensor
        def _(pe):
            for step, tri in enumerate(("before", "upto")):
                pe.wait_ge(dlink, 2 if step == 0 else 2 + 5 + 1)
                rhs = logf.rearrange("p t h -> p (t h)")
                nc.tensor.matmul(s.ps[0][:, :], s.c(tri), rhs, start=True, stop=True).then_inc(summed, 1)
                nc.tensor.matmul(s.ps[1][:, :], s.c("ones"), rhs, start=True, stop=True).then_inc(summed, 1)
            pe.wait_ge(dlink, 2 + 5 + 1 + 5)
            for c in range(4):
                for i in range(4):
                    mm = nc.tensor.transpose(s.ps[2 + c][0:H0, i * P:(i + 1) * P], s.kh[:, 4 * c + i, 0:H0], s.c("ident"))
                mm.then_inc(turned, 1)

        @block.sync
        def _(sp):
            sp.wait_ge(khT_ready, 4)
            sp.dma_start(d["khT"], khT).then_inc(kh_out, 16)
            sp.wait_ge(kh_out, 16)




def route_block(nc, s, d, layer):
    n = TILES * EXPERTS
    at = 0

    def scratch(width=n, dt=F32):
        nonlocal at
        at += width
        a = s.big_a[:, at - width:at]
        return a

    def te(a):
        return a.rearrange("p (t e) -> p t e", t=TILES)

    prob, big, tmp, rank, rd, wr = (te(scratch()) for _ in range(6))
    onehot = [te(scratch()) for _ in range(TOPK)]
    many = scratch(n // 2).bitcast(BF16).rearrange("p (t e) -> p t e", t=TILES)
    top = scratch(TILES * 8).rearrange("p (t k) -> p t k", t=TILES)
    arg = scratch(TILES * 8).bitcast(U32).rearrange("p (t k) -> p t k", t=TILES)
    argf = scratch(TILES * 8).rearrange("p (t k) -> p t k", t=TILES)
    base = scratch(n + EXPERTS).rearrange("p (t e) -> p t e", t=TILES + 1)
    tot = te(scratch())
    rowmax, rowsum = scratch(TILES), scratch(TILES)
    sum_a, sum_b, ntile, offset = (scratch(EXPERTS) for _ in range(4))
    ntile_i = scratch(EXPERTS).bitcast(I32)
    tile_col = scratch(1)

    def over_experts(a):
        return a.unsqueeze(2).to_broadcast([P, TILES, EXPERTS])

    def over_tiles(a):
        return a.unsqueeze(1).to_broadcast([P, TILES, EXPERTS])

    with signals(nc, f"r{layer}") as sem, ExitStack() as ctx:
        dlink, shifted, exped, top_done, many_ready, ranked, col_ready, row_done, slots_done = map(
            sem, ("dlink", "shifted", "exped", "top", "many", "ranked", "col", "row", "slots"))
        attn_in = sem("attn_in")
        block = ctx.enter_context(nc.Block())

        if layer == 1:
            @block.sync
            def _(sp):
                def load(name, src, shape=None):
                    dst = attn1_view(s, name)
                    sp.dma_start(dst if shape is None else dst.rearrange(shape, k=KC), src).then_inc(attn_in, 16)

                for name, src in (("wka", d["wka"]), ("wkb", d["wkb"]), ("wv", d["wv"])):
                    load(name, src.rearrange("(k p) n -> p k n", p=P), "p (k n) -> p k n")
                load("gath", d["wq1"].rearrange("(k p) n -> p k n", p=P), "p (k n) -> p k n")
                load("rotate", d["rotate1"])
                load("wo", d["wo1"])
                load("bv", d["bv1"].to_broadcast([P, P]))
                for name, src in (("bq", d["bq"]), ("bka", d["bka"]), ("bkb", d["bkb"])):
                    load(name, src)
                sp.wait_ge(attn_in, 16 * 10)

        @block.scalar
        def _(act):
            act.wait_ge(shifted, 1)
            nc.scalar.activation(prob, tmp, ACT.Exp).then_inc(exped, 1)

        @block.tensor
        def _(pe):
            pe.wait_ge(many_ready, 1)
            flat = many.rearrange("p t e -> p (t e)")
            nc.tensor.matmul(s.ps[0][:, :], s.beforeb[:], flat, start=True, stop=True)
            nc.tensor.matmul(s.ps[1][:, :], s.onesb[:], flat, start=True, stop=True).then_inc(ranked, 1)
            pe.wait_ge(col_ready, 1)
            nc.tensor.matmul(s.ps[2][0:1, 0:SLOT_TILES], tile_col[0:SLOT_TILES, :], s.c("ident")[0:SLOT_TILES, 0:SLOT_TILES],
                             start=True, stop=True).then_inc(row_done, 1)

        @block.vector
        def _(dve):
            link = Link(dve, dlink)
            v = nc.vector
            link(v.tensor_reduce(rowmax, s.logits[:], AX.X, ALU.max))
            v.tensor_tensor(tmp, s.logits[:], over_experts(rowmax), ALU.subtract).then_inc(shifted, 1)
            dve.wait_ge(exped, 1)
            for t in range(TILES):
                v.max(top[:, t, :], prob[:, t, :]).then_inc(top_done, 1)
            for t in range(TILES):
                dve.wait_ge(top_done, t + 1)
                ins = v.max_index(arg[:, t, :], top[:, t, :], prob[:, t, :])
            link(ins)
            link(v.tensor_reduce(rowsum, top[:, :, 0:TOPK], AX.X, ALU.add))
            link(v.reciprocal(rowsum, rowsum))
            link(v.tensor_tensor(s.weight[:], top[:, :, 0:TOPK],
                                 rowsum.unsqueeze(2).to_broadcast([P, TILES, TOPK]), ALU.mult))
            link(v.tensor_copy(argf, arg))
            for k in range(TOPK):
                ins = v.tensor_tensor(onehot[k], over_tiles(s.c("iota")), over_experts(argf[:, :, k]), ALU.is_equal)
            link(ins)
            link(v.tensor_tensor(tmp, onehot[0], onehot[1], ALU.add))
            link(v.tensor_tensor(big, onehot[2], onehot[3], ALU.add))
            v.tensor_tensor(many, tmp, big, ALU.add).then_inc(many_ready, 1)
            link(v.memset(base[:, 0, :], 0.0))
            dve.wait_ge(ranked, 1)
            link(v.tensor_copy(tot, te(s.ps[1][:, :])))
            for t in range(TILES):
                link(v.tensor_tensor(base[:, t + 1, :], base[:, t, :], tot[:, t, :], ALU.add))
            count = base[:, TILES, :]
            if layer == 1:
                link(v.tensor_scalar(count, count, float(CAP1), None, ALU.min))
            link(v.tensor_scalar(ntile_i, count, float(P - 1), None, ALU.add))
            link(v.tensor_scalar(ntile_i, ntile_i, 7, None, ALU.arith_shift_right))
            link(v.tensor_copy(ntile, ntile_i))
            a, b = ntile, sum_a
            for sh in (1, 2, 4, 8, 16):
                v.tensor_copy(b[:, 0:sh], a[:, 0:sh])
                link(v.tensor_tensor(b[:, sh:], a[:, sh:], a[:, 0:EXPERTS - sh], ALU.add))
                a, b = b, (sum_b if b is sum_a else sum_a)
            link(v.tensor_tensor(offset, a, ntile, ALU.subtract))
            link(v.tensor_scalar(offset, offset, float(P), None, ALU.mult))
            link(v.tensor_scalar(b, a, s.c("index"), None, ALU.is_le))
            link(v.tensor_reduce(tile_col, b, AX.X, ALU.add))
            v.tensor_scalar(tile_col, tile_col, float(EXPERTS - 1), None, ALU.min).then_inc(col_ready, 1)
            link(v.tensor_copy(rank, te(s.ps[0][:, :])))
            link(v.tensor_tensor(rank, rank, base[:, 0:TILES, :], ALU.add))
            if layer == 0:
                link(v.tensor_tensor(rd, rank, over_tiles(offset), ALU.add))
            else:
                link(v.tensor_scalar(wr, rank, float(CAP1), float(OUT_OF_RANGE), ALU.is_ge, ALU.mult))
                link(v.tensor_scalar(rank, rank, float(CAP1 - 1), None, ALU.min))
                link(v.tensor_tensor(rd, rank, over_tiles(offset), ALU.add))
                link(v.tensor_tensor(wr, wr, rd, ALU.add))
            for k in range(TOPK):
                link(v.tensor_tensor(tmp, onehot[k], rd, ALU.mult))
                link(v.tensor_reduce(rowsum, tmp, AX.X, ALU.add))
                link(v.tensor_copy(s.slot_r[:, k, :], rowsum))
                if layer == 1:
                    link(v.tensor_tensor(tmp, onehot[k], wr, ALU.mult))
                    link(v.tensor_reduce(rowsum, tmp, AX.X, ALU.add))
                    link(v.tensor_copy(s.slot_w[:, k, :], rowsum))
            dve.wait_ge(row_done, 1)
            link(v.tensor_copy(s.tile_expert[:], s.ps[2][0:1, 0:SLOT_TILES]))


def scatter_tile(nc, s, d, layer, t, scattered):
    slot = s.slot_r if layer == 0 else s.slot_w
    for k in range(TOPK):
        nc.gpsimd.indirect_dma_start(
            out=d["xs"], out_offset=bass.IndirectOffsetOnAxis(ap=slot[:, k, t:t + 1], axis=0),
            in_=s.xn[:, t, :], in_offset=None, bounds_check=SLOTS - 1, oob_is_err=False,
        ).then_inc(scattered[k], 16)



ROW_AT = [0, P, 3 * P, 6 * P]
COL_AT = [0, 4 * P, 7 * P, 9 * P]
SCORE_BANK = [(1, 384), (2, 0), (1, 0), (0, 0)]
ORDER = (3, 2, 0, 1)
BANK_FULL = {3: 1, 2: 3, 0: 3, 1: 4}
TURN_BANK = [(3, 0), (4, 0), (5, 0), (4, 384)]


def attention_block0(nc, s, d, rows, extra):
    NU = len(rows) * H0
    with signals(nc, f"a{rows[0]}") as sem, ExitStack() as ctx:
        q_done, rope_part, q_ready, k_ready = map(sem, ("q_done", "rope_part", "q_ready", "k_ready"))
        scored, maxed, exped, rsum_ready, prob_ready = map(sem, ("scored", "maxed", "exped", "rsum", "prob"))
        turned, out_v, out_a, weighted, o_ready = map(sem, ("turned", "outv", "outa", "weighted", "o_ready"))
        wout_done, x_added = map(sem, ("wout_done", "x_added"))
        w_in = [sem(f"wq_in{i}") for i in range(2)]
        kh_in = [sem(f"kh_in{i}") for i in range(2)]
        gathered = [sem(f"gathered{i}") for i in range(UNROLL)]
        gu_in = sem("gu_in")
        block = ctx.enter_context(nc.Block())

        def heads(eng, step, between, drain):
            for bi in range(len(rows)):
                step(bi * H0, bi, 0, 0)
                if bi:
                    between(bi - 1)
                step(bi * H0 + 1, bi, 1, 1)
                with eng.Fori(1, H0 // 2 - 1) as r:
                    for par in range(2):
                        step(bi * H0 + 2 * r + par, bi, 2 * r + par, par)
                for h in (H0 - 2, H0 - 1):
                    step(bi * H0 + h, bi, h, h % 2)
            drain()
            between(len(rows) - 1)

        def next_row(bi, h):
            if isinstance(h, int) and h >= H0 - 2:
                return bi + 1 if bi + 1 < len(rows) else None
            return bi

        def loads(u, par):
            return 8 * (u - par) + 16

        combining = extra == "combine"

        def adds_before(bi, h):
            n = ROWS * bi if not (isinstance(h, int) and h == 0) else ROWS * max(bi - 1, 0)
            return n + (2 * (bi * H0 + h) if combining and bi < 2 else (2 * 2 * H0 if combining else 0))

        def wout_count(bi, i):
            if not combining:
                done = 0
            else:
                done = min(2 * ((bi + 1) * H0 + 1), 4 * H0) if bi + 1 < len(rows) else 4 * H0
                done = min(done, 4 * H0)
            return ROWS * bi + done + i + 1

        def choice_added(t, bi, k):
            h = 2 * (t - 8 * bi) + k // 2
            return adds_before(bi, h) + k % 2 + 1

        @block.sync
        def _(sp):
            def load(u, bi, h, par):
                if not (isinstance(u, int) and u < 2):
                    sp.wait_ge(q_done, u - 1)
                sp.dma_start(s.wq[:, par], d["wq0"].rearrange("(h k p) n -> p h k n", k=KC, p=P)[:, bass.ds(h, 1)].rearrange(
                    "p a k n -> p (a k) n")).then_inc(w_in[par], 16)
                if not (isinstance(u, int) and u < 2):
                    sp.wait_ge(k_ready, u - 1)
                b = rows[bi]
                sp.dma_start(s.khb[:, par], d["khT"][bass.ds(h, 1), b * SEQ:(b + 1) * SEQ].to_broadcast([P, SEQ])
                             ).then_inc(kh_in[par], 16)

            heads(sp, load, lambda _: None, lambda: None)
            if extra == "scatter":
                sp.dma_start(s.gu0, d["gu0"].rearrange("(k p) n -> p k n", p=P)).then_inc(gu_in, 16)
                sp.wait_ge(gu_in, 16)

        @block.gpsimd
        def _(pool):
            def operands(u, bi, par):
                pool.wait_ge(kh_in[par], loads(u, par))
                if not (isinstance(u, int) and u < 2):
                    pool.wait_ge(scored, ROWS * (u - 1))
                b = rows[bi]
                nc.gpsimd.tensor_tensor(s.kT[:, par], s.kpT[:, b * SEQ:(b + 1) * SEQ], s.khb[:, par],
                                        ALU.mult).then_inc(k_ready, 1)
                pool.wait_ge(rope_part, u + 1)
                nc.gpsimd.tensor_tensor(s.qT[:, par], s.rope_a, s.rope_b, ALU.add).then_inc(q_ready, 1)

            for u in range(NU):
                operands(u, u // H0, u % 2)
                if extra == "scatter":
                    scatter_tile(nc, s, d, 0, u, gathered)
                elif 1 <= u <= 2 * TILES:
                    t = (u - 1) // 2
                    for k in (2 * ((u - 1) % 2), 2 * ((u - 1) % 2) + 1):
                        if t:
                            pool.wait_ge(x_added, choice_added(t - 1, (t - 1) // 8, k))
                        nc.gpsimd.indirect_dma_start(
                            out=s.gath[0][:, k], out_offset=None, in_=d["ys"],
                            in_offset=bass.IndirectOffsetOnAxis(ap=s.slot_r[:, k, t:t + 1], axis=0),
                        ).then_inc(gathered[k], 16)
            if extra == "scatter":
                for k in range(TOPK):
                    pool.wait_ge(gathered[k], 16 * TILES)

        @block.tensor
        def _(pe):
            def query(u, bi, par):
                pe.wait_ge(w_in[par], loads(u, par))
                if not (isinstance(u, int) and u == 0):
                    pe.wait_ge(rope_part, u)
                b = rows[bi]
                for k in range(KC):
                    mm = nc.tensor.matmul(s.ps[6][:, :], s.wq[:, par, k, :], s.xnT[:, k, b * SEQ:(b + 1) * SEQ],
                                          start=k == 0, stop=k == KC - 1)
                mm.then_inc(q_done, 1)

            def scores(u, par):
                pe.wait_ge(q_ready, u + 1)
                pe.wait_ge(k_ready, u + 1)
                if not (isinstance(u, int) and u == 0):
                    pe.wait_ge(exped, ROWS * u)
                for i in ORDER:
                    bank, at = SCORE_BANK[i]
                    w = (i + 1) * P
                    nc.tensor.matmul(s.ps[bank][:, at:at + w], s.qT[:, par, i * P:(i + 1) * P], s.kT[:, par, 0:w],
                                     start=True, stop=False)
                    nc.tensor.matmul(s.ps[bank][:, at + w - P:at + w], s.identb[:], s.maskb[:],
                                     start=False, stop=True).then_inc(scored, 1)

            def turn(u, par):
                pe.wait_ge(prob_ready, ROWS * u + ROWS)
                if not (isinstance(u, int) and u == 0):
                    pe.wait_ge(out_v, u)
                    pe.wait_ge(out_a, (ROWS - 1) * u)
                for j in (0, 1, 3, 2):
                    bank, at = TURN_BANK[j]
                    for i in range(j, ROWS):
                        mm = nc.tensor.transpose(s.ps[bank][:, at + (i - j) * P:at + (i - j + 1) * P],
                                                 s.probs[:, par, ROW_AT[i] + j * P:ROW_AT[i] + (j + 1) * P], s.c("ident"))
                    mm.then_inc(turned, 1)

            def values(u, bi):
                if not (isinstance(u, int) and u == 0):
                    pe.wait_ge(o_ready, u)
                pe.wait_ge(out_v, u + 1)
                pe.wait_ge(out_a, (ROWS - 1) * (u + 1))
                for j in range(ROWS):
                    w = (ROWS - j) * P
                    mm = nc.tensor.matmul(s.ps[7][:, j * P:], s.vp[:, rows[bi] * ROWS + j, :],
                                          s.probsT[:, COL_AT[j]:COL_AT[j] + w], start=j == 0, stop=j == ROWS - 1)
                mm.then_inc(weighted, 1)

            def step(u, bi, h, par):
                scores(u, par)
                first = isinstance(u, int) and u == 0
                if not first:
                    turn(u - 1, 1 - par)
                ahead = next_row(bi, h)
                if ahead is not None:
                    query(u + 2, ahead, par)
                if not first:
                    values(u - 1, bi - 1 if isinstance(h, int) and h == 0 else bi)

            def project(bi):
                pe.wait_ge(o_ready, H0 * (bi + 1))
                for i in range(ROWS):
                    bank = 3 + i % 2
                    if i >= 2:
                        pe.wait_ge(x_added, wout_count(bi, i - 2))
                    else:
                        pe.wait_ge(out_v, H0 * (bi + 1))
                        pe.wait_ge(out_a, (ROWS - 1) * H0 * (bi + 1))
                    for h in range(H0):
                        mm = nc.tensor.matmul(s.ps[bank][:, 0:EMB], s.oT[:, h, i * P:(i + 1) * P], s.wout[:, h, :],
                                              start=h == 0, stop=h == H0 - 1)
                    mm.then_inc(wout_done, 1)
                    pe.wait_ge(wout_done, ROWS * bi + i + 1)
                pe.wait_ge(x_added, wout_count(bi, ROWS - 1))

            def drain():
                u = NU - 1
                turn(u, 1)
                values(u, len(rows) - 1)

            query(0, 0, 0)
            query(1, 0, 1)
            heads(pe, step, project, drain)

        @block.vector
        def _(dve):
            v = nc.vector

            def rotate(u, par):
                dve.wait_ge(q_done, u + 1)
                if not (isinstance(u, int) and u == 0):
                    dve.wait_ge(q_ready, u)
                rope0(nc, s, s.ps[6]).then_inc(rope_part, 1)

            def maxima(u, par):
                for n, i in enumerate(ORDER):
                    bank, at = SCORE_BANK[i]
                    dve.wait_ge(scored, ROWS * u + BANK_FULL[i])
                    if n == 0 and not (isinstance(u, int) and u < 2):
                        dve.wait_ge(exped, ROWS * (u - 1))
                    v.tensor_reduce(s.negmax[:, par, i:i + 1], s.ps[bank][:, at:at + (i + 1) * P], AX.X, ALU.max,
                                    negate=True).then_inc(maxed, 1)

            def normalise(u, par):
                dve.wait_ge(exped, ROWS * (u + 1))
                if not (isinstance(u, int) and u < 2):
                    dve.wait_ge(prob_ready, ROWS * (u - 1))
                v.reciprocal(s.rsum[:, par], s.psumrow[:, par]).then_inc(rsum_ready, 1)
                dve.wait_ge(rsum_ready, u + 1)
                for i in reversed(range(ROWS)):
                    row = s.probs[:, par, ROW_AT[i]:ROW_AT[i] + (i + 1) * P]
                    v.tensor_scalar(row, row, s.rsum[:, par, i:i + 1], None, ALU.mult).then_inc(prob_ready, 1)

            def out0(u, bi, h):
                dve.wait_ge(turned, ROWS * u + 1)
                if not (isinstance(u, int) and u == 0):
                    dve.wait_ge(weighted, u)
                bank, at = TURN_BANK[0]
                v.tensor_scalar(s.probsT[:, COL_AT[0]:COL_AT[0] + SEQ], s.ps[bank][:, 0:SEQ],
                                s.kh[:, rows[bi] * ROWS, bass.ds(H0 + h, 1)], None, ALU.mult).then_inc(out_v, 1)

            def combine(u, bi, h, par):
                n = adds_before(bi, h)
                for kk in range(2):
                    k = 2 * par + kk
                    t = 8 * bi + (h // 2 if isinstance(h, int) else (h - par) // 2)
                    dve.wait_ge(gathered[k], 16 * (t + 1))
                    if not (isinstance(n, int) and n == 0 and kk == 0):
                        dve.wait_ge(x_added, n + kk)
                    xt = s.x[:, bass.ds(t, 1), :].rearrange("p a e -> p (a e)")
                    v.scalar_tensor_tensor(out=xt, in0=s.gath[0][:, k], scalar=s.weight[:, bass.ds(t, 1), k],
                                           in1=xt, op0=ALU.mult, op1=ALU.add).then_inc(x_added, 1)

            def step(u, bi, h, par):
                maxima(u, par)
                if not (isinstance(u, int) and u == 0):
                    if isinstance(h, int) and h == 0:
                        out0(u - 1, bi - 1, H0 - 1)
                    else:
                        out0(u - 1, bi, h - 1)
                normalise(u, par)
                if next_row(bi, h) is not None:
                    rotate(u + 2, par)
                if combining and bi < 2:
                    combine(u, bi, h, par)

            def project(bi):
                for i in range(ROWS):
                    t = rows[bi] * ROWS + i
                    dve.wait_ge(wout_done, ROWS * bi + i + 1)
                    if wout_count(bi, i) > 1:
                        dve.wait_ge(x_added, wout_count(bi, i) - 1)
                    v.tensor_tensor(s.x[:, t, :], s.ps[3 + i % 2][:, 0:EMB], s.x[:, t, :], ALU.add).then_inc(x_added, 1)

            rotate(0, 0)
            rotate(1, 1)
            heads(dve, step, project, lambda: out0(NU - 1, len(rows) - 1, H0 - 1))

        @block.scalar
        def _(act):
            def exps(u, par):
                for n, i in enumerate(ORDER):
                    bank, at = SCORE_BANK[i]
                    act.wait_ge(maxed, ROWS * u + BANK_FULL[i])
                    if n == 0 and not (isinstance(u, int) and u < 2):
                        act.wait_ge(turned, ROWS * (u - 1))
                    nc.scalar.activation(s.probs[:, par, ROW_AT[i]:ROW_AT[i] + (i + 1) * P],
                                         s.ps[bank][:, at:at + (i + 1) * P], ACT.Exp,
                                         bias=s.negmax[:, par, i:i + 1],
                                         accum_out=s.psumrow[:, par, i:i + 1]).then_inc(exped, 1)

            def outs(u, bi, h):
                if not (isinstance(u, int) and u == 0):
                    act.wait_ge(weighted, u)
                for n, j in enumerate((1, 3, 2)):
                    bank, at = TURN_BANK[j]
                    w = (ROWS - j) * P
                    act.wait_ge(turned, ROWS * u + (3 if n < 2 else 4))
                    nc.scalar.activation(s.probsT[:, COL_AT[j]:COL_AT[j] + w], s.ps[bank][:, at:at + w], ACT.Copy,
                                         scale=s.kh[:, rows[bi] * ROWS + j, bass.ds(H0 + h, 1)]).then_inc(out_a, 1)

            def heads_out(u, bi, h):
                act.wait_ge(weighted, u + 1)
                if bi > 0 and isinstance(h, int) and h == 0:
                    act.wait_ge(wout_done, ROWS * bi)
                nc.scalar.activation(s.oT[:, bass.ds(h, 1)].rearrange("p a n -> p (a n)"), s.ps[7][:, :],
                                     ACT.Copy).then_inc(o_ready, 1)

            def step(u, bi, h, par):
                exps(u, par)
                if isinstance(u, int) and u == 0:
                    return
                if isinstance(h, int) and h == 0:
                    outs(u - 1, bi - 1, H0 - 1)
                    heads_out(u - 1, bi - 1, H0 - 1)
                else:
                    outs(u - 1, bi, h - 1)
                    heads_out(u - 1, bi, h - 1)

            def drain():
                outs(NU - 1, len(rows) - 1, H0 - 1)
                heads_out(NU - 1, len(rows) - 1, H0 - 1)

            heads(act, step, lambda _: None, drain)




def expert_block(nc, s, d, layer):
    inter = I0 if layer == 0 else I1
    gu, dn = (s.gu0, s.dn0) if layer == 0 else (s.gu1, s.dn1)
    W = 2 * inter
    rows_in = s.probs[:].rearrange("p a n -> p (a n)")[:, 0:UNROLL * EMB].rearrange("p (j e) -> p j e", j=UNROLL)
    rowsT = s.probsT[:, 0:2 * EMB].rearrange("p (j n) -> p j n", j=2)
    outs = s.rope[:].rearrange("p a (b e) -> p (a b) e", e=EMB)
    silu = s.qT[:, :, 0:inter]
    hid = s.kT[:, :, 0:inter]
    hidT = s.khb[:, :, 0:P]
    with signals(nc, f"e{layer}") as sem, ExitStack() as ctx:
        turned, rowsT_ready, gu_done, silu_done, hid_ready, hid_turned, hidT_ready, down_done, out_ready = map(
            sem, ("turned", "rowsT", "gu_done", "silu", "hid", "hid_turned", "hidT", "down", "out"))
        w_in = sem("w_in")
        x_in = [sem(f"x_in{j}") for j in range(UNROLL)]
        y_out = [sem(f"y_out{j}") for j in range(UNROLL)]
        block = ctx.enter_context(nc.Block())
        N = SLOT_TILES

        def known(i):
            return isinstance(i, int)

        def tiles(eng, step, tail):
            for i in range(UNROLL):
                step(i, i)
            with eng.Fori(1, N // UNROLL - 1) as r:
                for j in range(UNROLL):
                    step(UNROLL * r + j, j)
            for i in range(N - UNROLL, N + tail):
                step(i, i % UNROLL)

        @block.sync
        def _(sp):
            if layer == 0:
                sp.dma_start(dn, d["dn0"]).then_inc(w_in, 16)

            def load(i, j):
                if not (known(i) and i < UNROLL):
                    sp.wait_ge(turned, i - UNROLL + 1)
                sp.dma_start(rows_in[:, j], d["xs"][bass.ds(i * P, P), :]).then_inc(x_in[j], 16)

            tiles(sp, load, 0)
            if layer == 0:
                sp.wait_ge(w_in, 16)

        @block.tensor
        def _(pe):
            def turn_rows(i, j):
                pe.wait_ge(x_in[j], 4 * (i - j) + 16)
                if not (known(i) and i < 2):
                    pe.wait_ge(rowsT_ready, i - 1)
                for k in range(KC):
                    mm = nc.tensor.transpose(s.ps[j % 2][:, k * P:(k + 1) * P], rows_in[:, j, k * P:(k + 1) * P],
                                             s.c("ident"))
                mm.then_inc(turned, 1)

            expert = [pe.alloc_register(f"expert{j}_e{layer}") for j in range(UNROLL)]

            def read_expert(i, j):
                pe.reg_load(expert[j], s.tile_expert[0:1, bass.ds(i, 1)])

            def gate_up(i, j):
                e = pe.snap(expert[j], min_val=0, max_val=EXPERTS - 1)
                pe.wait_ge(rowsT_ready, i + 1)
                if not (known(i) and i < 2):
                    pe.wait_ge(hid_ready, i - 1)
                for k in range(KC):
                    mm = nc.tensor.matmul(s.ps[2 + j % 2][:, 0:W], rowsT[:, j % 2, k * P:(k + 1) * P],
                                          gu[:, k, bass.ds(e * W, W)], start=k == 0, stop=k == KC - 1)
                mm.then_inc(gu_done, 1)

            def turn_hidden(i, j):
                pe.wait_ge(hid_ready, i + 1)
                if not (known(i) and i < 2):
                    pe.wait_ge(hidT_ready, i - 1)
                nc.tensor.transpose(s.ps[4 + j % 2][0:inter, 0:P], hid[:, j % 2, :], s.c("ident")).then_inc(hid_turned, 1)

            def down(i, j):
                e = pe.snap(expert[j], min_val=0, max_val=EXPERTS - 1)
                pe.wait_ge(hidT_ready, i + 1)
                if not (known(i) and i < 2):
                    pe.wait_ge(out_ready, i - 1)
                nc.tensor.matmul(s.ps[6 + j % 2][:, 0:EMB], hidT[0:inter, j % 2, :], dn[0:inter, bass.ds(e * EMB, EMB)],
                                 start=True, stop=True).then_inc(down_done, 1)

            def step(i, j):
                if not known(i) or i < N:
                    gate_up(i, j)
                if not known(i) or i + 1 < N:
                    turn_rows(i + 1, (j + 1) % UNROLL)
                if not known(i) or 2 <= i < N + 2:
                    down(i - 2, (j - 2) % UNROLL)
                if not known(i) or i + 2 < N:
                    read_expert(i + 2, (j + 2) % UNROLL)
                if not known(i) or 1 <= i < N + 1:
                    turn_hidden(i - 1, (j - 1) % UNROLL)

            read_expert(0, 0)
            read_expert(1, 1)
            turn_rows(0, 0)
            if layer == 0:
                pe.wait_ge(w_in, 16)
            tiles(pe, step, 2)

        @block.scalar
        def _(act):
            def gate(i, j):
                act.wait_ge(gu_done, i + 1)
                if not (known(i) and i < 2):
                    act.wait_ge(hid_ready, i - 1)
                nc.scalar.activation(silu[:, j % 2, :], s.ps[2 + j % 2][:, 0:inter], ACT.Silu).then_inc(silu_done, 1)

            def out(i, j):
                act.wait_ge(down_done, i + 1)
                if not (known(i) and i < UNROLL):
                    act.wait_ge(y_out[j], 4 * (i - j))
                nc.scalar.activation(outs[:, j], s.ps[6 + j % 2][:, 0:EMB], ACT.Copy).then_inc(out_ready, 1)
                act.wait_ge(out_ready, i + 1)
                act.dma_start(d["ys"][bass.ds(i * P, P), :], outs[:, j]).then_inc(y_out[j], 16)

            def step(i, j):
                if not known(i) or i < N:
                    gate(i, j)
                if not known(i) or 2 <= i < N + 2:
                    out(i - 2, (j - 2) % UNROLL)

            tiles(act, step, 2)
            for j in range(UNROLL):
                act.wait_ge(y_out[j], 16 * N // UNROLL)

        @block.vector
        def _(dve):
            v = nc.vector

            def rowsT_out(i, j):
                dve.wait_ge(turned, i + 1)
                if not (known(i) and i < 2):
                    dve.wait_ge(gu_done, i - 1)
                v.tensor_copy(rowsT[:, j % 2, :], s.ps[j % 2][:, 0:EMB]).then_inc(rowsT_ready, 1)

            def hidden(i, j):
                dve.wait_ge(silu_done, i + 1)
                if not (known(i) and i < 2):
                    dve.wait_ge(hid_turned, i - 1)
                v.tensor_tensor(hid[:, j % 2, :], silu[:, j % 2, :], s.ps[2 + j % 2][:, inter:W], ALU.mult).then_inc(hid_ready, 1)

            def hidT_out(i, j):
                dve.wait_ge(hid_turned, i + 1)
                if not (known(i) and i < 2):
                    dve.wait_ge(down_done, i - 1)
                v.tensor_copy(hidT[0:inter, j % 2, :], s.ps[4 + j % 2][0:inter, 0:P]).then_inc(hidT_ready, 1)

            def step(i, j):
                if not known(i) or i + 1 < N:
                    rowsT_out(i + 1, (j + 1) % UNROLL)
                if not known(i) or i < N:
                    hidden(i, j)
                if not known(i) or 1 <= i < N + 1:
                    hidT_out(i - 1, (j - 1) % UNROLL)

            rowsT_out(0, 0)
            tiles(dve, step, 2)




TAIL1 = KC * EXPERTS * 2 * I1
_ATTN1 = dict(gath=UNROLL * EMB, rotate=3 * SEQ, wka=KC * P, wkb=KC * P, wv=KC * P, wo=EMB, bv=P, bq=GROUPS1,
              bka=1, bkb=1, wqs=KC * P, bqs=1)


def attn1_view(s, name):
    at = TAIL1
    for n, w in _ATTN1.items():
        if n == name:
            return s.big_a[:, at:at + w]
        at += w
    raise KeyError(name)


def norm_block1(nc, s, d):
    xn1 = s.big_a[:, TAIL1:TAIL1 + TILES * EMB].rearrange("p (t e) -> p t e", t=TILES)
    xfT = s.big_b[:, 0:KC * TOKENS].rearrange("p (k n) -> p k n", k=KC)
    w = s.probs[:].rearrange("p a n -> p (a n)")
    bo, nw, gate = w[:, 0:EMB], w[:, EMB:2 * EMB], w[:, 512:512 + KC * EXPERTS].rearrange("p (k n) -> p k n", k=KC)
    sg, su = (w[:, at:at + KC * I1].rearrange("p (k n) -> p k n", k=KC) for at in (640, 896))
    sd = w[:, 1152:1152 + EMB]
    square = s.kT[:, 0, 0:EMB]
    rms = s.kh[:, 0, 0:TILES]
    silu, hid = s.rope, s.qT
    GU_BANKS = [(4, 5), (0, 1)]
    DOWN_BANKS = [6, 3]
    CHUNKS = TOKENS // SEQ
    with signals(nc, "n1") as sem, ExitStack() as ctx:
        w_in, stat, aggr, var_ready, std_ready, rstd_ready, xn_ready = map(
            sem, ("w_in", "stat", "aggr", "var", "std", "rstd", "xn"))
        squared, ms_ready, rms_std, rms_ready, xf_ready, x_added = map(
            sem, ("squared", "ms", "rms_std", "rms", "xf", "x_added"))
        turned_n, xnT_ready, turned_f, xfT_ready, gated, silu_done, hid_ready, down_done, logits_done, logits_out = map(
            sem, ("turned_n", "xnT", "turned_f", "xfT", "gated", "silu", "hid", "down", "logits_done", "logits_out"))
        block = ctx.enter_context(nc.Block())

        @block.sync
        def _(sp):
            def kchunks(a):
                return a.rearrange("(k p) n -> p k n", p=P)

            sp.dma_start(bo, d["bo1"].to_broadcast([P, EMB])).then_inc(w_in, 16)
            sp.dma_start(nw, d["normw1"].to_broadcast([P, EMB])).then_inc(w_in, 16)
            sp.dma_start(gate, kchunks(d["gate1"])).then_inc(w_in, 16)
            sp.dma_start(sg, kchunks(d["sg1"])).then_inc(w_in, 16)
            sp.dma_start(su, kchunks(d["su1"])).then_inc(w_in, 16)
            sp.dma_start(sd, d["sd1"]).then_inc(w_in, 16)
            sp.wait_ge(w_in, 96)

        @block.vector
        def _(dve):
            v = nc.vector
            for t in range(TILES):
                v.bn_stats(s.stats[:, t, :], s.x[:, t, :]).then_inc(stat, 1)
            for t in range(TILES):
                dve.wait_ge(stat, t + 1)
                v.bn_aggr(s.meanvar[:, t, :], s.stats[:, t, :]).then_inc(aggr, 1)
            dve.wait_ge(aggr, TILES)
            v.tensor_scalar(s.rstd[:], s.meanvar[:, :, 1], 1e-5, None, ALU.add).then_inc(var_ready, 1)
            dve.wait_ge(std_ready, 1)
            v.reciprocal(s.rstd[:], s.rstd[:]).then_inc(rstd_ready, 1)
            dve.wait_ge(rstd_ready, 1)
            for t in range(TILES):
                v.tensor_scalar(xn1[:, t, :], s.x[:, t, :], s.meanvar[:, t, 0:1], s.rstd[:, t:t + 1],
                                ALU.subtract, ALU.mult).then_inc(xn_ready, 1)
            link = Link(dve, x_added)
            dve.wait_ge(xn_ready, TILES)
            link(v.tensor_tensor(s.x[:], s.x[:], xn1, ALU.add))
            dve.wait_ge(w_in, 96)
            link(v.tensor_tensor(s.x[:], s.x[:], bo.unsqueeze(1).to_broadcast([P, TILES, EMB]), ALU.add))
            for g in range(TILES // 4 * KC):
                dve.wait_ge(turned_n, g + 1)
                v.tensor_copy(s.xnT[:, g % KC, g // KC * 512:(g // KC + 1) * 512], s.ps[g % 4][:, :]).then_inc(xnT_ready, 1)
            dve.wait_ge(squared, TILES)
            v.tensor_scalar(rms, rms, 1.0 / EMB, 1e-6, ALU.mult, ALU.add).then_inc(ms_ready, 1)
            dve.wait_ge(rms_std, 1)
            v.reciprocal(rms, rms).then_inc(rms_ready, 1)
            dve.wait_ge(rms_ready, 1)
            for t in range(TILES):
                v.scalar_tensor_tensor(out=s.xn[:, t, :], in0=xn1[:, t, :], scalar=rms[:, t:t + 1], in1=nw,
                                       op0=ALU.mult, op1=ALU.mult).then_inc(xf_ready, 1)

            def add_down(c):
                for half in range(2):
                    dve.wait_ge(down_done, 2 * c + half + 1)
                    t = 4 * c + 2 * half
                    link(v.tensor_tensor(s.x[:, t:t + 2, :], s.x[:, t:t + 2, :],
                                         s.ps[DOWN_BANKS[half]][:, :].rearrange("p (t e) -> p t e", t=2), ALU.add))

            for c in range(CHUNKS):
                dve.wait_ge(silu_done, c + 1)
                if c >= 2:
                    dve.wait_ge(down_done, 2 * (c - 1))
                v.tensor_tensor(hid[:, c % 2], silu[:, c % 2], s.ps[GU_BANKS[c % 2][1]][:, :], ALU.mult).then_inc(hid_ready, 1)
                if c:
                    add_down(c - 1)
            add_down(CHUNKS - 1)
            dve.wait_ge(logits_done, 1)
            v.tensor_copy(s.logits[:], s.ps[7][:, :].rearrange("p (t e) -> p t e", t=TILES)).then_inc(logits_out, 1)

        @block.scalar
        def _(act):
            a = nc.scalar.activation
            act.wait_ge(var_ready, 1)
            a(s.rstd[:], s.rstd[:], ACT.Sqrt).then_inc(std_ready, 1)
            for t in range(TILES):
                act.wait_ge(xn_ready, t + 1)
                if t:
                    act.wait_ge(squared, t)
                a(square, xn1[:, t, :], ACT.Square, accum_out=rms[:, t:t + 1]).then_inc(squared, 1)
            act.wait_ge(ms_ready, 1)
            a(rms, rms, ACT.Sqrt).then_inc(rms_std, 1)
            for g in range(TILES // 4 * KC):
                act.wait_ge(turned_f, g + 1)
                a(xfT[:, g % KC, g // KC * 512:(g // KC + 1) * 512], s.ps[g % 4][:, :], ACT.Copy).then_inc(xfT_ready, 1)
            for c in range(CHUNKS):
                act.wait_ge(gated, c + 1)
                if c >= 2:
                    act.wait_ge(hid_ready, c - 1)
                a(silu[:, c % 2], s.ps[GU_BANKS[c % 2][0]][:, :], ACT.Silu).then_inc(silu_done, 1)

        @block.tensor
        def _(pe):
            groups = TILES // 4 * KC
            for src, ready, turned, taken, before in ((xn1, xn_ready, turned_n, xnT_ready, None),
                                                      (s.xn, xf_ready, turned_f, xfT_ready, xnT_ready)):
                for g in range(groups):
                    c, k = g // KC, g % KC
                    pe.wait_ge(ready, 4 * c + 4)
                    if g >= 4:
                        pe.wait_ge(taken, g - 3)
                    elif before is not None:
                        pe.wait_ge(before, groups - 3 + g)
                    for i in range(4):
                        mm = nc.tensor.transpose(s.ps[g % 4][:, i * P:(i + 1) * P],
                                                 src[:, 4 * c + i, k * P:(k + 1) * P], s.c("ident"))
                    mm.then_inc(turned, 1)
            pe.wait_ge(w_in, 96)
            pe.wait_ge(xfT_ready, groups)
            for t in range(TILES):
                for k in range(KC):
                    mm = nc.tensor.matmul(s.ps[7][:, t * EXPERTS:(t + 1) * EXPERTS], xfT[:, k, t * P:(t + 1) * P],
                                          gate[:, k, :], start=k == 0, stop=k == KC - 1)
            mm.then_inc(logits_done, 1)

            def gate_up(c):
                if c >= 2:
                    pe.wait_ge(hid_ready, c - 1)
                for bank, wt in zip(GU_BANKS[c % 2], (sg, su)):
                    for k in range(KC):
                        mm = nc.tensor.matmul(s.ps[bank][:, :], wt[:, k, :], xfT[:, k, c * SEQ:(c + 1) * SEQ],
                                              start=k == 0, stop=k == KC - 1)
                mm.then_inc(gated, 1)

            def down(c):
                pe.wait_ge(hid_ready, c + 1)
                for half in range(2):
                    if c:
                        pe.wait_ge(x_added, 2 + 2 * (c - 1) + half + 1)
                    for i in range(2):
                        mm = nc.tensor.matmul(s.ps[DOWN_BANKS[half]][:, i * EMB:(i + 1) * EMB],
                                              hid[:, c % 2, (2 * half + i) * P:(2 * half + i + 1) * P], sd,
                                              start=True, stop=True)
                    mm.then_inc(down_done, 1)

            gate_up(0)
            for c in range(CHUNKS):
                if c + 1 < CHUNKS:
                    gate_up(c + 1)
                down(c)




def attention_block1(nc, s, d, rows, extra):
    NU = len(rows) * H1
    part = lambda name: attn1_view(s, name)
    kchunk = lambda a: a.rearrange("p (k n) -> p k n", k=KC)
    rotate = part("rotate").rearrange("p (a n) -> p a n", a=3)
    wqs, wka, wkb, wv = (kchunk(part(n)) for n in ("wqs", "wka", "wkb", "wv"))
    bqs, bka, bkb, bv, wo = (part(n) for n in ("bqs", "bka", "bkb", "bv", "wo"))
    raw_q = part("gath").rearrange("p (k g n) -> p k g n", k=KC, g=GROUPS1)
    values = s.khb[:].rearrange("p a (i n) -> p a i n", i=ROWS)
    headsT = s.wq[:].rearrange("p a k n -> p (a k n)")
    gath = s.big_a[:, 0:TILES * TOPK * EMB].rearrange("p (j e) -> p j e", j=TILES * TOPK)
    scattering = extra == "scatter"
    with signals(nc, f"c{rows[0]}") as sem, ExitStack() as ctx:
        summed, projected, proj_out, k_ready = map(sem, ("summed", "projected", "proj_out", "k_ready"))
        scored, maxed, exped, rsum_ready, prob_ready = map(sem, ("scored", "maxed", "exped", "rsum", "prob"))
        turned, out_v, out_a, weighted, heads_ready, wo_done, x_added = map(
            sem, ("turned", "outv", "outa", "weighted", "heads", "wo_done", "x_added"))
        moved = [sem(f"moved{i}") for i in range(TOPK)]
        gathered = [] if scattering else [sem(f"gathered{t}") for t in range(TILES)]
        w_in, y_stored = sem("w_in"), sem("y_stored")
        block = ctx.enter_context(nc.Block())
        PROJ = 4

        order = []
        left = [("row", t, k) for t in range(TILES) for k in range(TOPK)] if not scattering else []
        for u in range(NU):
            if u % H1 == 0 and u:
                order.append((u, [("wo", u // H1 - 1, half) for half in range(2)]))
            if u >= 2:
                order.append((u, left[:4]))
                left = left[4:]
        order.append((NU, [("wo", len(rows) - 1, half) for half in range(2)] + left))
        flat = [x for _, xs in order for x in xs]
        count_of = {x: n + 1 for n, x in enumerate(flat)}

        @block.sync
        def _(sp):
            if scattering:
                sp.dma_start(s.gu1, d["gu1"].rearrange("(k p) n -> p k n", p=P)).then_inc(w_in, 16)
                sp.dma_start(s.dn1, d["dn1"]).then_inc(w_in, 16)
                sp.wait_ge(w_in, 32)
            else:
                out = d["out"].rearrange("(t p) e -> p t e", p=P)
                for g in range(TILES // 2):
                    last = [count_of["row", t, k] for t in (2 * g, 2 * g + 1) for k in range(TOPK)]
                    b, i = 2 * g // ROWS, 2 * g % ROWS
                    if b in rows:
                        last.append(count_of["wo", rows.index(b), i // 2])
                    sp.wait_ge(x_added, max(last))
                    sp.dma_start(out[:, 2 * g:2 * g + 2], s.x[:, 2 * g:2 * g + 2]).then_inc(y_stored, 16)
                sp.wait_ge(y_stored, 16 * TILES // 2)

        @block.gpsimd
        def _(pool):
            if scattering:
                for t in range(TILES):
                    scatter_tile(nc, s, d, 1, t, moved)
                for k in range(TOPK):
                    pool.wait_ge(moved[k], 16 * TILES)
            else:
                for t in range(TILES):
                    for k in range(TOPK):
                        nc.gpsimd.indirect_dma_start(
                            out=gath[:, t * TOPK + k], out_offset=None, in_=d["ys"],
                            in_offset=bass.IndirectOffsetOnAxis(ap=s.slot_r[:, k, t:t + 1], axis=0),
                        ).then_inc(gathered[t], 16)

        @block.tensor
        def _(pe):
            def project(bi):
                b = rows[bi]
                cols = slice(b * SEQ, (b + 1) * SEQ)
                for n, wt in enumerate((wqs, wka, wkb)):
                    if bi or n:
                        pe.wait_ge(proj_out, PROJ * bi + n)
                    for k in range(KC):
                        mm = nc.tensor.matmul(s.ps[6][:, :], wt[:, k, :], s.xnT[:, k, cols], start=k == 0, stop=k == KC - 1)
                    mm.then_inc(projected, 1)
                pe.wait_ge(proj_out, PROJ * bi + 3)
                for i in range(ROWS):
                    for k in range(KC):
                        mm = nc.tensor.matmul(s.ps[6][:, i * P:(i + 1) * P], s.xnT[:, k, b * SEQ + i * P:b * SEQ + (i + 1) * P],
                                              wv[:, k, :], start=k == 0, stop=k == KC - 1)
                mm.then_inc(projected, 1)

            def scores(u):
                bi, h = divmod(u, H1)
                pe.wait_ge(k_ready, bi + 1)
                if u:
                    pe.wait_ge(exped, ROWS * u)
                lanes = slice(h * HP1, (h + 1) * HP1)
                for i in ORDER:
                    bank, at = SCORE_BANK[i]
                    w = (i + 1) * P
                    nc.tensor.matmul(s.ps[bank][:, at:at + w], s.qT[lanes, bi % 2, i * P:(i + 1) * P],
                                     s.kT[lanes, bi % 2, 0:w], start=True, stop=False)
                    nc.tensor.matmul(s.ps[bank][:, at + w - P:at + w], s.identb[:], s.maskb[:],
                                     start=False, stop=True).then_inc(scored, 1)

            def turn(u):
                pe.wait_ge(prob_ready, ROWS * u + ROWS)
                if u:
                    pe.wait_ge(out_v, u)
                    pe.wait_ge(out_a, (ROWS - 1) * u)
                for j in (0, 1, 3, 2):
                    bank, at = TURN_BANK[j]
                    for i in range(j, ROWS):
                        mm = nc.tensor.transpose(s.ps[bank][:, at + (i - j) * P:at + (i - j + 1) * P],
                                                 s.probs[:, u % 2, ROW_AT[i] + j * P:ROW_AT[i] + (j + 1) * P], s.c("ident"))
                    mm.then_inc(turned, 1)

            def weigh(u):
                bi, h = divmod(u, H1)
                if h == 0 and bi:
                    pe.wait_ge(heads_ready, bi)
                pe.wait_ge(proj_out, PROJ * (bi + 1))
                pe.wait_ge(out_v, u + 1)
                pe.wait_ge(out_a, (ROWS - 1) * (u + 1))
                lanes = slice(h * HP1, (h + 1) * HP1)
                for j in range(ROWS):
                    mm = nc.tensor.matmul(s.ps[7][lanes, j * P:], values[:, bi % 2, j, lanes],
                                          s.probsT[:, COL_AT[j]:COL_AT[j] + (ROWS - j) * P], start=j == 0, stop=j == ROWS - 1)
                mm.then_inc(weighted, 1)

            def out(bi):
                pe.wait_ge(heads_ready, bi + 1)
                pe.wait_ge(out_v, H1 * (bi + 1))
                pe.wait_ge(out_a, (ROWS - 1) * H1 * (bi + 1))
                for half in range(2):
                    for i in range(2):
                        t = 2 * half + i
                        mm = nc.tensor.matmul(s.ps[3 + half][:, i * EMB:(i + 1) * EMB], headsT[:, t * P:(t + 1) * P], wo,
                                              start=True, stop=True)
                    mm.then_inc(wo_done, 1)
                pe.wait_ge(x_added, count_of["wo", bi, 1])

            if scattering:
                pe.wait_ge(summed, 6)
            project(0)
            for u in range(NU):
                scores(u)
                if u:
                    turn(u - 1)
                if u % H1 == 1 and u // H1 + 1 < len(rows):
                    project(u // H1 + 1)
                if u:
                    weigh(u - 1)
                if u % H1 == 0 and u:
                    out(u // H1 - 1)
            turn(NU - 1)
            weigh(NU - 1)
            out(len(rows) - 1)

        @block.vector
        def _(dve):
            v = nc.vector
            if scattering:
                link = Link(dve, summed)
                link(v.tensor_tensor(wqs, raw_q[:, :, 0], raw_q[:, :, 1], ALU.add))
                link(v.tensor_tensor(wqs, wqs, raw_q[:, :, 2], ALU.add))
                link(v.tensor_tensor(wqs, wqs, raw_q[:, :, 3], ALU.add))
                link(v.tensor_tensor(bqs, part("bq")[:, 0:1], part("bq")[:, 1:2], ALU.add))
                link(v.tensor_tensor(bqs, bqs, part("bq")[:, 2:3], ALU.add))
                link(v.tensor_tensor(bqs, bqs, part("bq")[:, 3:4], ALU.add))

            def take(bi):
                par = bi % 2
                if bi >= 2:
                    dve.wait_ge(scored, ROWS * H1 * (bi - 1))
                for n, (dst, bias) in enumerate(((s.qT[:, par], bqs), (s.rope_a, bka), (s.rope_b, bkb))):
                    dve.wait_ge(projected, PROJ * bi + n + 1)
                    if n and bi:
                        dve.wait_ge(k_ready, bi)
                    ins = v.scalar_tensor_tensor(out=dst, in0=s.ps[6][:, :], scalar=bias, in1=rotate[:, n], op0=ALU.add,
                                                 op1=ALU.mult)
                    ins.then_inc(proj_out, 1)
                dve.wait_ge(proj_out, PROJ * bi + 3)
                v.tensor_tensor(s.kT[:, par], s.rope_a, s.rope_b, ALU.add).then_inc(k_ready, 1)
                dve.wait_ge(projected, PROJ * bi + PROJ)
                v.tensor_tensor(values[:, par], s.ps[6][:, :].rearrange("p (i n) -> p i n", i=ROWS),
                                bv.unsqueeze(1).to_broadcast([P, ROWS, P]), ALU.add).then_inc(proj_out, 1)

            def maxima(u):
                for n, i in enumerate(ORDER):
                    bank, at = SCORE_BANK[i]
                    dve.wait_ge(scored, ROWS * u + BANK_FULL[i])
                    if n == 0 and u >= 2:
                        dve.wait_ge(exped, ROWS * (u - 1))
                    v.tensor_reduce(s.negmax[:, u % 2, i:i + 1], s.ps[bank][:, at:at + (i + 1) * P], AX.X, ALU.max,
                                    negate=True).then_inc(maxed, 1)

            def normalise(u):
                dve.wait_ge(exped, ROWS * (u + 1))
                if u >= 2:
                    dve.wait_ge(prob_ready, ROWS * (u - 1))
                v.reciprocal(s.rsum[:, u % 2], s.psumrow[:, u % 2]).then_inc(rsum_ready, 1)
                dve.wait_ge(rsum_ready, u + 1)
                for i in reversed(range(ROWS)):
                    row = s.probs[:, u % 2, ROW_AT[i]:ROW_AT[i] + (i + 1) * P]
                    v.tensor_scalar(row, row, s.rsum[:, u % 2, i:i + 1], None, ALU.mult).then_inc(prob_ready, 1)

            def out0(u):
                dve.wait_ge(turned, ROWS * u + 1)
                if u:
                    dve.wait_ge(weighted, u)
                v.tensor_copy(s.probsT[:, 0:SEQ], s.ps[TURN_BANK[0][0]][:, 0:SEQ]).then_inc(out_v, 1)

            done = [0]

            def additions(u):
                for at, what in order:
                    if at != u:
                        continue
                    for x in what:
                        kind, a, k = x
                        if done[0]:
                            dve.wait_ge(x_added, done[0])
                        if kind == "wo":
                            dve.wait_ge(wo_done, 2 * a + k + 1)
                            t = rows[a] * ROWS + 2 * k
                            ins = v.tensor_tensor(s.x[:, t:t + 2, :], s.x[:, t:t + 2, :],
                                                  s.ps[3 + k][:, :].rearrange("p (t e) -> p t e", t=2), ALU.add)
                        else:
                            dve.wait_ge(gathered[a], 16 * TOPK)
                            ins = v.scalar_tensor_tensor(out=s.x[:, a, :], in0=gath[:, a * TOPK + k],
                                                         scalar=s.weight[:, a, k:k + 1], in1=s.x[:, a, :],
                                                         op0=ALU.mult, op1=ALU.add)
                        ins.then_inc(x_added, 1)
                        done[0] += 1

            take(0)
            for u in range(NU):
                maxima(u)
                if u:
                    out0(u - 1)
                if u % H1 == 1 and u // H1 + 1 < len(rows):
                    take(u // H1 + 1)
                normalise(u)
                additions(u)
            out0(NU - 1)
            additions(NU)

        @block.scalar
        def _(act):
            def exps(u):
                for n, i in enumerate(ORDER):
                    bank, at = SCORE_BANK[i]
                    act.wait_ge(maxed, ROWS * u + BANK_FULL[i])
                    if n == 0 and u >= 2:
                        act.wait_ge(turned, ROWS * (u - 1))
                    nc.scalar.activation(s.probs[:, u % 2, ROW_AT[i]:ROW_AT[i] + (i + 1) * P],
                                         s.ps[bank][:, at:at + (i + 1) * P], ACT.Exp, bias=s.negmax[:, u % 2, i:i + 1],
                                         accum_out=s.psumrow[:, u % 2, i:i + 1]).then_inc(exped, 1)

            def outs(u):
                if u:
                    act.wait_ge(weighted, u)
                for n, j in enumerate((1, 3, 2)):
                    bank, at = TURN_BANK[j]
                    w = (ROWS - j) * P
                    act.wait_ge(turned, ROWS * u + (3 if n < 2 else 4))
                    nc.scalar.activation(s.probsT[:, COL_AT[j]:COL_AT[j] + w], s.ps[bank][:, at:at + w],
                                         ACT.Copy).then_inc(out_a, 1)
                bi, h = divmod(u, H1)
                if h == H1 - 1:
                    act.wait_ge(weighted, u + 1)
                    if bi:
                        act.wait_ge(wo_done, 2 * bi)
                    nc.scalar.activation(headsT, s.ps[7][:, :], ACT.Copy).then_inc(heads_ready, 1)

            for u in range(NU):
                exps(u)
                if u:
                    outs(u - 1)
            outs(NU - 1)




def constants():
    i = np.arange(P)
    c = np.zeros((P, CONST_W), np.float32)

    def put(name, v):
        a, b = const_at(name)
        c[:, a:b] = v

    put("ident", np.eye(P))
    put("before", i[:, None] < i[None, :])
    put("upto", i[:, None] <= i[None, :])
    put("ones", 1.0)
    put("mask", np.where(i[None, :] > i[:, None], MASKED, 0.0))
    put("iota", np.arange(EXPERTS)[None, :])
    put("index", i[:, None])
    pos = np.arange(SEQ, dtype=np.float32)
    inv = (np.float32(10000.0) ** (-np.arange(0, D0, 2, dtype=np.float32) / D0)).astype(np.float32)
    ang = inv[:, None] * pos[None, :]
    put("cos0", np.tile(np.cos(ang), (2, 1)))
    put("sin0", np.concatenate([np.sin(ang), -np.sin(ang)]))
    inv1 = (1.0 / np.float32(10000.0) ** (np.arange(D1 // 2, dtype=np.float32) * 2.0 / D1)).astype(np.float32)
    ang1 = inv1[:, None] * pos[None, :]
    co, si = np.cos(ang1), np.sin(ang1)
    rotate1 = [np.tile(np.concatenate(rows), (H1, 1)) for rows in (
        [co * D1 ** -0.5, co * D1 ** -0.5, si * D1 ** -0.5, si * D1 ** -0.5], [co, co, co, -co], [-si, si, si, si])]
    return c, np.concatenate(rotate1, axis=1).astype(np.float32)


def layout(inputs):
    w = {k: np.asarray(v) for k, v in inputs.items()}
    const, rotate1 = constants()
    out = {"const": const, "rotate1": rotate1, "x": w["L0_attn_x"].reshape(TOKENS, EMB)}
    kvT = w["L0_attn_Wkv"].T
    out["wcat0"] = np.concatenate([kvT[:, D0:], w["L0_attn_Wkvh"].T, w["L0_attn_Wg"].T, w["L0_ffn_gate"]], axis=1)
    out["wk0"] = kvT[:, 0:D0]
    out["wq0"] = w["L0_attn_Wq"].T.reshape(KC, P, H0, D0).transpose(2, 0, 1, 3).reshape(H0 * KC * P, D0)
    out["wout0"] = w["L0_attn_Wout"].T
    out["gu0"] = w["L0_ffn_gate_up_proj"].transpose(1, 0, 2).reshape(EMB, EXPERTS * 2 * I0)
    out["dn0"] = w["L0_ffn_down_proj"].transpose(1, 0, 2).reshape(I0, EXPERTS * EMB)
    half = D1 // 2
    first, second = 2 * np.arange(half), 2 * np.arange(half) + 1

    def spread(a, parts):
        picked = a[..., np.concatenate(parts)]
        return picked.reshape(*picked.shape[:-2], -1)

    wq = w["L1_attn_Wq"].reshape(EMB, H1, GROUPS1, D1).transpose(0, 2, 1, 3)
    out["wq1"] = spread(wq, [first, second, first, second]).reshape(EMB, GROUPS1 * P)
    bq = w["L1_attn_bq"].reshape(H1, GROUPS1, D1).transpose(1, 0, 2)
    out["bq"] = spread(bq, [first, second, first, second]).T
    wk, bk = w["L1_attn_Wk"].reshape(EMB, H1, D1), w["L1_attn_bk"].reshape(1, H1, D1)
    for name, parts in (("ka", [first, second, second, first]), ("kb", [second, first, first, second])):
        out["w" + name] = spread(wk, parts)
        out["b" + name] = spread(bk, parts).T
    def pad(a, axis):
        width = [(0, 0)] * a.ndim
        width[axis] = (0, HP1 - D1)
        return np.pad(a, width)

    out["wv"] = pad(w["L1_attn_Wv"].reshape(EMB, H1, D1), 2).reshape(EMB, P)
    out["bv1"] = pad(w["L1_attn_bv"].reshape(1, H1, D1), 2).reshape(1, P)
    out["wo1"] = pad(w["L1_attn_Wo"].reshape(H1, D1, EMB), 1).reshape(P, EMB)
    out["bo1"] = w["L1_attn_bo"].reshape(1, EMB)
    out["normw1"] = w["L1_ffn_norm_w"].reshape(1, EMB)
    out["gate1"] = w["L1_ffn_gate_w"].T
    out["gu1"] = w["L1_ffn_w13"].transpose(1, 0, 2).reshape(EMB, EXPERTS * 2 * I1)
    out["dn1"] = w["L1_ffn_w2"].transpose(1, 0, 2).reshape(I1, EXPERTS * EMB)
    out["sg1"], out["su1"], out["sd1"] = (w["L1_ffn_shared_gate_w"], w["L1_ffn_shared_up_w"], w["L1_ffn_shared_down_w"])
    return {k: np.ascontiguousarray(v) for k, v in out.items()}


def program(nc, d):
    with ExitStack() as ctx:
        s = make_buffers(nc, ctx)
        norm_block0(nc, s, d)
        gains_block0(nc, s, d)
        route_block(nc, s, d, 0)
        attention_block0(nc, s, d, [0], "scatter")
        expert_block(nc, s, d, 0)
        attention_block0(nc, s, d, [1, 2, 3], "combine")
        norm_block1(nc, s, d)
        route_block(nc, s, d, 1)
        attention_block1(nc, s, d, [0, 1], "scatter")
        expert_block(nc, s, d, 1)
        attention_block1(nc, s, d, [2, 3], "combine")


def kernel(**inputs):
    import concourse.bacc as bacc
    from concourse.bass_utils import run_bass_kernel_spmd

    arrays = layout(inputs)
    nc = bacc.Bacc("TRN2", target_bir_lowering=False, num_devices=1)
    d = {name: nc.dram_tensor(f"in_{name}", a.shape, mybir.dt.float32, kind="ExternalInput").ap()
         for name, a in arrays.items()}
    for name, shape in dict(khT=(H0, TOKENS), xs=(SLOTS, EMB), ys=(SLOTS, EMB)).items():
        d[name] = nc.dram_tensor(f"{name}_dram", shape, mybir.dt.float32).ap()
    d["out"] = nc.dram_tensor("out", (TOKENS, EMB), mybir.dt.float32, kind="ExternalOutput").ap()
    program(nc, d)
    result = run_bass_kernel_spmd(nc, [{f"in_{name}": a for name, a in arrays.items()}], core_ids=[0])
    return result.results[0]["out"].reshape(BATCH, SEQ, EMB)
```

```python
from contextlib import ExitStack, contextmanager

import numpy as np

import concourse.bass as bass
import concourse.mybir as mybir

F32 = mybir.dt.float32
F32R = mybir.dt.float32r
BF16 = mybir.dt.bfloat16
I32 = mybir.dt.int32
U32 = mybir.dt.uint32
ALU = mybir.AluOpType
ACT = mybir.ActivationFunctionType
AX = mybir.AxisListType

P = 128
BATCH, SEQ, EMB = 4, 512, 256
TOKENS = BATCH * SEQ
TILES = TOKENS // P
ROWS = SEQ // P
KC = EMB // P
EXPERTS, TOPK = 32, 4
SLOT_TILES = 96
SLOTS = SLOT_TILES * P
UNROLL = 4
STEPS = 8
EARLY_TILES = 6
CAP1 = 2 * TOKENS * TOPK // EXPERTS
OUT_OF_RANGE = 1 << 16
H0, D0, I0 = 16, 128, 96
H1, D1, I1 = 4, 16, 128
HP1 = 32
GROUPS1 = 4
MASKED = -1e30
PARTS_AT, PARTS_W = 4096, 2 * (2 * KC * SEQ + 2 * KC * P)

PV0, PKH0, PG0, PGATE0 = 0, D0, D0 + 2 * H0, D0 + 4 * H0
PROJ0 = PGATE0 + EXPERTS
_CONST = dict(ident=P, before=P, upto=P, ones=P, mask=P, iota=EXPERTS, index=1,
              cos0=SEQ, sin0=SEQ)


def const_at(name):
    at = 0
    for n, w in _CONST.items():
        if n == name:
            return at, at + w
        at += w
    raise KeyError(name)


CONST_W = sum(_CONST.values())


class Buffers:
    pass


def make_buffers(nc, ctx):
    s = Buffers()

    def sb(name, shape, dt=F32):
        t = ctx.enter_context(nc.sbuf_tensor(name, shape, dt))
        return t

    s.const = sb("const", [P, CONST_W])
    s.identb = sb("identb", [P, P], BF16)
    s.maskb = sb("maskb", [P, P], BF16)
    s.beforeb = sb("beforeb", [P, P], BF16)
    s.onesb = sb("onesb", [P, P], BF16)
    s.x = sb("x_res", [P, TILES, EMB])
    s.xn = sb("xn", [P, TILES, EMB])
    s.xnT = sb("xnT", [P, KC, TOKENS])
    big_a_at = nc.sbuf_base
    s.big_a = sb("big_a", [P, 80 * 256])
    s.parts = nc.alloc_sbuf_tensor_at("parts", [P, PARTS_W], F32R, offset=big_a_at + 4 * PARTS_AT)
    s.big_b = sb("big_b", [P, 32 * 256])
    s.probs = sb("probs", [P, 2, 1280])
    s.probsT = sb("probsT", [P, 1280])
    s.qT = sb("qT", [P, 2, SEQ])
    s.kT = sb("kT", [P, 2, SEQ])
    s.wq = sb("wq", [P, 2, KC, P])
    s.work = sb("work", [P, 4 * SEQ])
    s.rope, s.khb = (s.work[:, 2 * SEQ * i:2 * SEQ * (i + 1)].rearrange("p (a n) -> p a n", a=2) for i in range(2))
    s.rope_a, s.rope_b = s.rope[:, 0], s.rope[:, 1]
    s.kh = sb("kh", [P, TILES, 2 * H0])
    s.weight = sb("weight", [P, TILES, TOPK])
    s.slot_w = sb("slot_w", [P, TOPK, TILES], I32)
    s.slot_r = sb("slot_r", [P, TOPK, TILES], I32)
    s.tile_expert = sb("tile_expert", [1, SLOT_TILES], I32)
    s.logits = sb("logits", [P, TILES, EXPERTS])
    s.negmax = sb("negmax", [P, 2, ROWS])
    s.psumrow = sb("sumrow", [P, 2, ROWS])
    s.rsum = sb("rsum", [P, 2, ROWS])
    s.stats = sb("stats", [P, TILES, 6])
    s.meanvar = sb("meanvar", [P, TILES, 2])
    s.rstd = sb("rstd", [P, TILES])
    s.ps = [ctx.enter_context(nc.psum_tensor(f"bank{i}", [P, 512], F32)) for i in range(8)]

    def const(name):
        a, b = const_at(name)
        return s.const[:, a:b]

    s.c = const
    s.gu0 = s.big_a[:, 0:KC * EXPERTS * 2 * I0].rearrange("p (k n) -> p k n", k=KC)
    s.oT = s.big_a[:, 48 * 256:80 * 256].rearrange("p (h n) -> p h n", h=H0)
    s.dn0 = s.big_a[0:I0, 48 * 256:80 * 256]
    s.wout = s.big_b[:, 0:16 * 256].rearrange("p (h n) -> p h n", h=H0)
    s.kpT = s.big_b[:, 16 * 256:24 * 256]
    s.vp = s.big_b[:, 24 * 256:32 * 256].rearrange("p (t n) -> p t n", t=TILES)
    s.gu1 = s.big_a[:, 0:KC * EXPERTS * 2 * I1].rearrange("p (k n) -> p k n", k=KC)
    s.dn1 = s.big_b[:, :]
    s.gath = [s.big_a[:, at:at + UNROLL * EMB].rearrange("p (j e) -> p j e", j=UNROLL) for at in (0, 64 * 256)]
    return s


@contextmanager
def signals(nc, tag):
    made = []

    def sem(name):
        made.append(nc.alloc_semaphore(name=f"{name}_{tag}"))
        return made[-1]

    yield sem
    nc.clear_and_free_semaphores(made)
    nc.all_engine_barrier()


class Link:

    def __init__(self, eng, sem):
        self.eng, self.sem, self.n = eng, sem, 0

    def __call__(self, ins):
        self.n += 1
        ins.then_inc(self.sem, 1)
        self.eng.wait_ge(self.sem, self.n)




def norm_block0(nc, s, d, xs_zeroed):
    wcat = s.big_a[:, 0:KC * PROJ0].rearrange("p (k n) -> p k n", k=KC)
    wk = key_weights(s)
    zeros = s.big_a[:, 48 * 256:56 * 256]
    kg = s.big_a[:, 4096:4096 + TILES * 4 * H0].rearrange("p (t n) -> p t n", t=TILES)
    with signals(nc, "n0") as sem, ExitStack() as ctx:
        const_in, x_in, w_in, zero_made = map(sem, ("const_in", "x_in0", "w_in0", "zero_made"))
        cast, stat, aggr, var_ready, std_ready, rstd_ready, xn_ready = map(
            sem, ("cast", "stat0", "aggr0", "var0", "std0", "rstd0", "xn0"))
        turned, xnT_ready, proj_done, vp_out, kg_out = map(sem, ("turned0", "xnT0", "proj0", "vp_out", "kg_out"))
        x_ins = [x_in] + [sem(f"x_in0_{i}") for i in range(1, 4)]
        block = ctx.enter_context(nc.Block())

        @block.sync
        def _(sp):
            xv = d["x"].rearrange("(t p) e -> p t e", p=P)
            sp.dma_start(s.x[:, 0:4], xv[:, 0:4]).then_inc(x_ins[0], 16)
            small = const_at("cos0")[0]
            sp.dma_start(s.const[:, 0:small], d["const"][:, 0:small]).then_inc(const_in, 16)
            for c in range(1, 4):
                sp.dma_start(s.x[:, 4 * c:4 * c + 4], xv[:, 4 * c:4 * c + 4]).then_inc(x_ins[c], 16)
            sp.dma_start(wcat, d["wcat0"].rearrange("(k p) n -> p k n", p=P)).then_inc(w_in, 16)
            sp.dma_start(s.const[:, small:], d["const"][:, small:]).then_inc(w_in, 16)
            sp.dma_start(wk, d["wk0"].rearrange("(k p) n -> p k n", p=P)).then_inc(w_in, 16)
            sp.dma_start(s.wout, d["wout0"].rearrange("(h p) n -> p h n", p=P)).then_inc(w_in, 16)
            sp.wait_ge(zero_made, 1)
            xs = d["xs"].rearrange("(p r) e -> p (r e)", p=P)
            for c in range(12):
                sp.dma_start(xs[:, 2048 * c:2048 * (c + 1)], zeros).then_inc(xs_zeroed, 16)
            sp.wait_ge(w_in, 16 * 4)

        @block.gpsimd
        def _(pool):
            nc.gpsimd.memset(zeros, 0.0).then_inc(zero_made, 1)

        @block.vector
        def _(dve):
            def statistics(c):
                dve.wait_ge(x_ins[c], 16)
                for t in range(4 * c, 4 * c + 4):
                    nc.vector.bn_stats(s.stats[:, t, :], s.x[:, t, :]).then_inc(stat, 1)
                for t in range(4 * c, 4 * c + 4):
                    dve.wait_ge(stat, t + 1)
                    nc.vector.bn_aggr(s.meanvar[:, t, :], s.stats[:, t, :]).then_inc(aggr, 1)
                dve.wait_ge(aggr, 4 * c + 4)
                nc.vector.tensor_scalar(s.rstd[:, 4 * c:4 * c + 4], s.meanvar[:, 4 * c:4 * c + 4, 1], 1e-5, None,
                                        ALU.add).then_inc(var_ready, 1)

            def normalise(c):
                dve.wait_ge(std_ready, c + 1)
                rstd = s.rstd[:, 4 * c:4 * c + 4]
                nc.vector.reciprocal(rstd, rstd).then_inc(rstd_ready, 1)
                dve.wait_ge(rstd_ready, c + 1)
                for t in range(4 * c, 4 * c + 4):
                    nc.vector.tensor_scalar(s.xn[:, t, :], s.x[:, t, :], s.meanvar[:, t, 0:1], s.rstd[:, t:t + 1],
                                            ALU.subtract, ALU.mult).then_inc(xn_ready, 1)

            statistics(0)
            for c in range(1, 4):
                statistics(c)
                normalise(c - 1)
            dve.wait_ge(const_in, 16)
            nc.vector.tensor_copy(s.identb[:], s.c("ident")).then_inc(cast, 1)
            nc.vector.tensor_copy(s.maskb[:], s.c("mask")).then_inc(cast, 1)
            nc.vector.tensor_copy(s.beforeb[:], s.c("before")).then_inc(cast, 1)
            nc.vector.tensor_copy(s.onesb[:], s.c("ones")).then_inc(cast, 1)
            normalise(3)
            for g in range(TILES // 2):
                dve.wait_ge(proj_done, 2 * g + 2)
                src = s.ps[4 + g % 4][:, 0:2 * PROJ0].rearrange("p (t n) -> p t n", t=2)
                dve.wait_ge(vp_out, g + 1)
                nc.vector.tensor_copy(kg[:, 2 * g:2 * g + 2, :], src[:, :, PKH0:PGATE0]).then_inc(kg_out, 1)
                nc.vector.tensor_copy(s.logits[:, 2 * g:2 * g + 2, :], src[:, :, PGATE0:PROJ0]).then_inc(kg_out, 1)

        @block.scalar
        def _(act):
            for c in range(4):
                act.wait_ge(var_ready, c + 1)
                rstd = s.rstd[:, 4 * c:4 * c + 4]
                nc.scalar.activation(rstd, rstd, ACT.Sqrt).then_inc(std_ready, 1)
            for g in range(TILES // 4 * KC):
                act.wait_ge(turned, g + 1)
                nc.scalar.activation(s.xnT[:, g % KC, g // KC * 512:(g // KC + 1) * 512], s.ps[g % 4][:, :],
                                     ACT.Copy).then_inc(xnT_ready, 1)
            for g in range(TILES // 2):
                act.wait_ge(proj_done, 2 * g + 2)
                src = s.ps[4 + g % 4][:, 0:2 * PROJ0].rearrange("p (t n) -> p t n", t=2)
                nc.scalar.activation(s.vp[:, 2 * g:2 * g + 2, :], src[:, :, PV0:PV0 + D0], ACT.Copy).then_inc(vp_out, 1)

        @block.tensor
        def _(pe):
            pe.wait_ge(const_in, 16)
            for g in range(TILES // 4 * KC):
                c, k = g // KC, g % KC
                pe.wait_ge(xn_ready, 4 * c + 4)
                if g >= 4:
                    pe.wait_ge(xnT_ready, g - 3)
                for i in range(4):
                    mm = nc.tensor.transpose(s.ps[g % 4][:, i * P:(i + 1) * P],
                                             s.xn[:, 4 * c + i, k * P:(k + 1) * P], s.c("ident"))
                mm.then_inc(turned, 1)
            pe.wait_ge(w_in, 16 * 4)
            for t in range(TILES):
                pe.wait_ge(xnT_ready, KC * (t // 4) + KC)
                if t % 2 == 0 and t >= 8:
                    pe.wait_ge(kg_out, 2 * (t // 2 - 3))
                at = (t % 2) * PROJ0
                for k in range(KC):
                    mm = nc.tensor.matmul(s.ps[4 + t // 2 % 4][:, at:at + PROJ0], s.xnT[:, k, t * P:(t + 1) * P],
                                          wcat[:, k, :], start=k == 0, stop=k == KC - 1)
                mm.then_inc(proj_done, 1)


def key_weights(s):
    return s.big_a[:, 56 * 256:56 * 256 + KC * P].rearrange("p (k n) -> p k n", k=KC)


def rope0(nc, s, src):
    h = D0 // 2
    cos, sin = s.c("cos0"), s.c("sin0")
    nc.vector.tensor_tensor(s.rope_a, src[:, :], cos, ALU.mult)
    nc.vector.tensor_tensor(s.rope_b[h:, :], src[0:h, :], sin[0:h, :], ALU.mult)
    return nc.vector.tensor_tensor(s.rope_b[0:h, :], src[h:, :], sin[h:, :], ALU.mult)




GAIN_AT, PROJ_AT, ROUTE_AT = 0, 4096, 5120
TAIL1 = KC * EXPERTS * 2 * I1
_ATTN1 = dict(raw_q=KC * GROUPS1 * P, rotate=3 * SEQ, wka=KC * P, wkb=KC * P, wv=KC * P, wo=EMB, bv=P, bq=GROUPS1,
              bka=1, bkb=1, wqs=KC * P, bqs=1)


def attn1_view(s, name):
    at = TAIL1
    for n, w in _ATTN1.items():
        if n == name:
            return s.big_a[:, at:at + w]
        at += w
    raise KeyError(name)


def shared_weights(s):
    w = s.probs[:].rearrange("p a n -> p (a n)")
    at = 0
    views = []
    for width in (EMB, KC * EXPERTS, KC * I1, KC * I1, EMB):
        views.append(w[:, at:at + width])
        at += width
    nw, gate, sg, su, sd = views
    gate, sg, su = (a.rearrange("p (k n) -> p k n", k=KC) for a in (gate, sg, su))
    return nw, gate, sg, su, sd


def route_block(nc, s, d, layer, xs_zeroed=None):
    n = TILES * EXPERTS
    at = ROUTE_AT

    def scratch(width=n):
        nonlocal at
        at += width
        return s.big_a[:, at - width:at]

    def te(a):
        return a.rearrange("p (t e) -> p t e", t=TILES)

    def tk(a):
        return a.rearrange("p (t k) -> p t k", t=TILES)

    onehot = [te(scratch()) for _ in range(TOPK)]
    picked = [te(scratch()) for _ in range(TOPK)]
    pair = picked[0:2]
    rd, over = te(scratch()), te(scratch())
    many = scratch(n // 2).bitcast(BF16).rearrange("p (t e) -> p t e", t=TILES)
    top, arg, argf = tk(scratch(TILES * 8)), tk(scratch(TILES * 8).bitcast(U32)), tk(scratch(TILES * 8))
    slot_f, shifted_top = scratch(TOPK * TILES), tk(scratch(TOPK * TILES))
    rowsum = scratch(TILES)
    ntile_i, ntile = scratch(P).bitcast(I32)[0:EXPERTS, :], scratch(P)[0:EXPERTS, :]
    offset, ended = scratch(EXPERTS), scratch(EXPERTS)
    tile_col = scratch(1)
    assert at <= 48 * 256

    def over_experts(a):
        return a.unsqueeze(2).to_broadcast([P, TILES, EXPERTS])

    def over_tiles(a):
        return a.unsqueeze(1).to_broadcast([P, TILES, EXPERTS])

    RANK, small = s.ps[0], s.ps[1]
    COUNT, ENDS, TILE_ROW = small[0:EXPERTS, 0:P], small[:, P:P + 2 * EXPERTS], small[0:1, 2 * P:2 * P + SLOT_TILES]
    if layer == 0:
        ng = TILES * 2 * H0
        kg = s.big_a[:, PROJ_AT:PROJ_AT + TILES * 4 * H0].rearrange("p (t n) -> p t n", t=TILES)
        proj, gate = kg[:, :, 0:2 * H0], kg[:, :, 2 * H0:4 * H0]
        mag, logf, soft, cum = (te(s.big_a[:, GAIN_AT + i * ng:GAIN_AT + (i + 1) * ng]) for i in range(4))
        khT = s.probs[0:H0, :, :].rearrange("p a n -> p (a n)")[:, 0:TOKENS]
        SUMS = [s.ps[4], s.ps[5]]
        KEY_BANKS = [s.ps[2], s.ps[3]]
        wk = key_weights(s)
    else:
        _, _, sg, su, sd = shared_weights(s)
        xfT = s.big_b[:, 0:KC * TOKENS].rearrange("p (k n) -> p k n", k=KC)
        silu, hid = s.probsT[:, 0:2 * SEQ].rearrange("p (a n) -> p a n", a=2), s.khb
        rotate = attn1_view(s, "rotate").rearrange("p (a n) -> p a n", a=3)
        wqs, wka, wkb, wv = (attn1_view(s, a).rearrange("p (k n) -> p k n", k=KC) for a in ("wqs", "wka", "wkb", "wv"))
        bqs, bka, bkb, bv = (attn1_view(s, a) for a in ("bqs", "bka", "bkb", "bv"))
        UP_BANK, V_BANK, Q_BANK, KA_BANK, KB_BANK, GATE_BANK = s.ps[2:8]
        DOWN_BANKS = (RANK, small)

    with signals(nc, f"r{layer}") as sem, ExitStack() as ctx:
        row_read = sem("row_read")
        dlink, top_ready, weights_exp, many_ready, counted, ranked = map(
            sem, ("dlink", "top", "weights_exp", "many", "counted", "ranked"))
        ntile_ready, ends_done, col_ready, row_done, slots_done = map(sem, ("ntile", "ends", "col", "row", "slots"))
        logf_ready, soft_ready, summed, exp_ready, gained, kh_ready, kh_turned, khT_ready, kh_out = map(
            sem, ("logf", "soft", "summed", "expcum", "gained", "kh", "kh_turned", "khT", "kh_out"))
        alink, kp_done, kp_out, kp_ready = map(sem, ("alink", "kp_done", "kp_out", "kp_ready"))
        projected, taken, gated, silu_done, hid_ready, down_done, x_added = map(
            sem, ("projected", "taken", "gated", "silu", "hid", "down", "x_added"))
        moved = [sem(f"moved{k}") for k in range(TOPK)]
        block = ctx.enter_context(nc.Block())

        if layer == 0:
            @block.sync
            def _(sp):
                sp.wait_ge(khT_ready, 4)
                sp.dma_start(d["khT"], khT).then_inc(kh_out, 16)
                sp.wait_ge(kh_out, 16)
                sp.wait_ge(xs_zeroed, 16 * 12)

        @block.gpsimd
        def _(pool):
            if layer == 0:
                h = D0 // 2
                cos, sin = s.c("cos0"), s.c("sin0")
                link = Link(pool, kp_ready)
                for b in range(BATCH):
                    kp = s.kpT[:, b * SEQ:(b + 1) * SEQ]
                    pool.wait_ge(kp_out, b + 1)
                    link(nc.gpsimd.tensor_tensor(s.rope_a, kp, cos, ALU.mult))
                    link(nc.gpsimd.tensor_tensor(s.rope_b[h:, :], kp[0:h, :], sin[0:h, :], ALU.mult))
                    link(nc.gpsimd.tensor_tensor(s.rope_b[0:h, :], kp[h:, :], sin[h:, :], ALU.mult))
                    link(nc.gpsimd.tensor_tensor(kp, s.rope_a, s.rope_b, ALU.add))
            else:
                pool.wait_ge(slots_done, 1)
                for t in range(EARLY_TILES):
                    scatter_tile(nc, s, d, 1, t, moved)
                for k in range(TOPK):
                    pool.wait_ge(moved[k], 16 * EARLY_TILES)

        @block.scalar
        def _(act):
            a = nc.scalar.activation

            def weights():
                act.wait_ge(top_ready, 1)
                a(shifted_top, shifted_top, ACT.Exp).then_inc(weights_exp, 1)

            if layer == 0:
                act.wait_ge(logf_ready, 1)
                link = Link(act, alink)
                link(a(mag, mag, ACT.Exp))
                a(soft, mag, ACT.Ln, bias=1.0).then_inc(soft_ready, 1)
                for b in range(BATCH):
                    act.wait_ge(kp_done, b + 1)
                    a(s.kpT[:, b * SEQ:(b + 1) * SEQ], KEY_BANKS[b % 2][:, :], ACT.Copy).then_inc(kp_out, 1)
                weights()
                act.wait_ge(summed, 1)
                a(cum, te(SUMS[0][:, :]), ACT.Exp).then_inc(exp_ready, 1)
                act.wait_ge(summed, 2)
                a(s.kh[:], te(SUMS[1][:, :]), ACT.Copy).then_inc(kh_ready, 1)
                for c in range(4):
                    act.wait_ge(kh_turned, c + 1)
                    a(khT[:, c * 512:(c + 1) * 512], s.ps[4 + c][0:H0, :], ACT.Copy, scale=D0 ** -0.5).then_inc(khT_ready, 1)
            else:
                weights()
                for c in range(BATCH):
                    act.wait_ge(gated, c + 1)
                    if c >= 2:
                        act.wait_ge(hid_ready, c - 1)
                    a(silu[:, c % 2], GATE_BANK[:, :], ACT.Silu).then_inc(silu_done, 1)

        @block.tensor
        def _(pe):
            def count_and_rank():
                pe.wait_ge(many_ready, 1)
                for t in range(TILES):
                    mm = nc.tensor.matmul(COUNT[:, :], many[:, t, :], s.onesb[:], start=t == 0, stop=t == TILES - 1)
                mm.then_inc(counted, 1)
                flat = many.rearrange("p t e -> p (t e)")
                nc.tensor.matmul(RANK[:, :], s.beforeb[:], flat, start=True, stop=False)
                for j in range(1, TILES):
                    mm = nc.tensor.matmul(RANK[:, j * EXPERTS:], s.onesb[:], flat[:, 0:n - j * EXPERTS],
                                          start=False, stop=j == TILES - 1)
                mm.then_inc(ranked, 1)

            def ends():
                pe.wait_ge(ntile_ready, 1)
                nc.tensor.matmul(ENDS[:, :], ntile, s.c("before")[0:EXPERTS, 0:2 * EXPERTS],
                                 start=True, stop=True).then_inc(ends_done, 1)

            def tile_row():
                pe.wait_ge(col_ready, 1)
                nc.tensor.matmul(TILE_ROW[:, :], tile_col[0:SLOT_TILES, :], s.c("ident")[0:SLOT_TILES, 0:SLOT_TILES],
                                 start=True, stop=True).then_inc(row_done, 1)

            def running_sum(step, tri):
                def by_row(a):
                    return a.rearrange("p (b i h) -> p b i h", b=BATCH, i=ROWS)

                flat = logf.rearrange("p t h -> p (t h)")
                nc.tensor.matmul(SUMS[step][:, :], s.c(tri), flat, start=True, stop=False)
                for b in range(BATCH):
                    for j in range(1, ROWS):
                        w, at = 2 * H0, b * ROWS * 2 * H0
                        mm = nc.tensor.matmul(SUMS[step][:, at + j * w:at + ROWS * w], s.c("ones"),
                                              flat[:, at:at + (ROWS - j) * w], start=False,
                                              stop=b == BATCH - 1 and j == ROWS - 1)
                mm.then_inc(summed, 1)

            if layer == 0:
                for b in range(BATCH):
                    if b >= 2:
                        pe.wait_ge(kp_out, b - 1)
                    for k in range(KC):
                        mm = nc.tensor.matmul(KEY_BANKS[b % 2][:, :], wk[:, k, :], s.xnT[:, k, b * SEQ:(b + 1) * SEQ],
                                              start=k == 0, stop=k == KC - 1)
                    mm.then_inc(kp_done, 1)
                pe.wait_ge(logf_ready, 2)
                running_sum(0, "before")
                count_and_rank()
                ends()
                pe.wait_ge(gained, 1)
                running_sum(1, "upto")
                pe.wait_ge(kh_ready, 1)
                for c in range(4):
                    for i in range(4):
                        mm = nc.tensor.transpose(s.ps[4 + c][0:H0, i * P:(i + 1) * P], s.kh[:, 4 * c + i, 0:H0], s.c("ident"))
                    mm.then_inc(kh_turned, 1)
                tile_row()
                return

            def project(b):
                cols = slice(b * SEQ, (b + 1) * SEQ)
                for i, (wt, bank) in enumerate(((wqs, Q_BANK), (wka, KA_BANK), (wkb, KB_BANK))):
                    if b:
                        pe.wait_ge(taken, 4 * (b - 1) + i + 1)
                    for k in range(KC):
                        mm = nc.tensor.matmul(bank[:, :], wt[:, k, :], s.xnT[:, k, cols], start=k == 0, stop=k == KC - 1)
                if b:
                    pe.wait_ge(taken, 4 * b)
                for i in range(ROWS):
                    for k in range(KC):
                        mm = nc.tensor.matmul(V_BANK[:, i * P:(i + 1) * P], s.xnT[:, k, b * SEQ + i * P:b * SEQ + (i + 1) * P],
                                              wv[:, k, :], start=k == 0, stop=k == KC - 1)
                mm.then_inc(projected, 1)

            def gate_up(c):
                if c:
                    pe.wait_ge(hid_ready, c)
                for bank, wt in ((GATE_BANK, sg), (UP_BANK, su)):
                    for k in range(KC):
                        mm = nc.tensor.matmul(bank[:, :], wt[:, k, :], xfT[:, k, c * SEQ:(c + 1) * SEQ],
                                              start=k == 0, stop=k == KC - 1)
                mm.then_inc(gated, 1)

            def down(c):
                pe.wait_ge(hid_ready, c + 1)
                for half, bank in enumerate(DOWN_BANKS):
                    if c:
                        pe.wait_ge(x_added, 2 * (c - 1) + half + 1)
                    for i in range(2):
                        mm = nc.tensor.matmul(bank[:, i * EMB:(i + 1) * EMB],
                                              hid[:, c % 2, (2 * half + i) * P:(2 * half + i + 1) * P], sd,
                                              start=True, stop=True)
                    mm.then_inc(down_done, 1)

            project(0)
            count_and_rank()
            ends()
            gate_up(0)
            tile_row()
            for b in range(1, BATCH):
                project(b)
                if b == 1:
                    pe.wait_ge(row_read, 1)
                down(b - 1)
                gate_up(b)
            down(BATCH - 1)

        @block.vector
        def _(dve):
            link = Link(dve, dlink)
            v = nc.vector

            def take(b):
                dve.wait_ge(projected, b + 1)
                cols = slice(b * SEQ, (b + 1) * SEQ)
                for i, (dst, bank, bias) in enumerate(((s.xnT[:, 0, cols], Q_BANK, bqs), (s.rope_a, KA_BANK, bka),
                                                       (s.rope_b, KB_BANK, bkb))):
                    v.scalar_tensor_tensor(out=dst, in0=bank[:, :], scalar=bias, in1=rotate[:, i], op0=ALU.add,
                                           op1=ALU.mult).then_inc(taken, 1)
                v.tensor_tensor(values1(s)[b], V_BANK[:, :].rearrange("p (i n) -> p i n", i=ROWS),
                                bv.unsqueeze(1).to_broadcast([P, ROWS, P]), ALU.add).then_inc(taken, 1)
                dve.wait_ge(taken, 4 * b + 3)
                link(v.tensor_tensor(s.xnT[:, 1, cols], s.rope_a, s.rope_b, ALU.add))

            def hidden(c):
                dve.wait_ge(silu_done, c + 1)
                if c >= 2:
                    dve.wait_ge(down_done, 2 * (c - 1))
                v.tensor_tensor(hid[:, c % 2], silu[:, c % 2], UP_BANK[:, :], ALU.mult).then_inc(hid_ready, 1)

            def add_down(c):
                for half, bank in enumerate(DOWN_BANKS):
                    dve.wait_ge(down_done, 2 * c + half + 1)
                    t = 4 * c + 2 * half
                    v.tensor_tensor(s.x[:, t:t + 2, :], s.x[:, t:t + 2, :],
                                    bank[:, :].rearrange("p (t e) -> p t e", t=2), ALU.add).then_inc(x_added, 1)

            if layer == 0:
                v.scalar_tensor_tensor(out=mag, in0=gate, scalar=-1.0, in1=gate, op0=ALU.mult,
                                       op1=ALU.min).then_inc(logf_ready, 1)
                link(v.tensor_scalar(logf, gate, 0.0, None, ALU.min))
            for t in range(TILES):
                ins = v.max(top[:, t, :], s.logits[:, t, :])
            link(ins)
            for t in range(TILES):
                ins = v.max_index(arg[:, t, :], top[:, t, :], s.logits[:, t, :])
            if layer == 0:
                dve.wait_ge(soft_ready, 1)
                v.tensor_tensor(logf, logf, soft, ALU.subtract).then_inc(logf_ready, 1)
            link(ins)
            v.tensor_tensor(shifted_top, top[:, :, 0:TOPK], top[:, :, 0:1].to_broadcast([P, TILES, TOPK]),
                            ALU.subtract).then_inc(top_ready, 1)
            link(v.tensor_copy(argf, arg))
            for k in range(TOPK):
                ins = v.tensor_tensor(onehot[k], over_tiles(s.c("iota")), over_experts(argf[:, :, k]), ALU.is_equal)
                if k % 2:
                    link(ins)
                    ins = v.tensor_tensor(pair[k // 2], onehot[k - 1], onehot[k], ALU.add)
                    if k == TOPK - 1:
                        link(ins)
            v.tensor_tensor(many, pair[0], pair[1], ALU.add).then_inc(many_ready, 1)
            if layer == 0:
                dve.wait_ge(exp_ready, 1)
                v.tensor_tensor(logf, proj, cum, ALU.mult).then_inc(gained, 1)
            if layer == 1:
                take(0)
            dve.wait_ge(counted, 1)
            rows = COUNT[:, :]
            if layer == 0:
                link(v.tensor_scalar(ntile_i, rows, float(P - 1), None, ALU.add))
            else:
                link(v.tensor_scalar(ntile_i, rows, float(CAP1), float(P - 1), ALU.min, ALU.add))
            link(v.tensor_scalar(ntile_i, ntile_i, 7, None, ALU.arith_shift_right))
            v.tensor_copy(ntile, ntile_i).then_inc(ntile_ready, 1)
            dve.wait_ge(weights_exp, 1)
            link(v.tensor_reduce(rowsum, shifted_top, AX.X, ALU.add))
            link(v.reciprocal(rowsum, rowsum))
            v.tensor_tensor(s.weight[:], shifted_top, rowsum.unsqueeze(2).to_broadcast([P, TILES, TOPK]), ALU.mult)
            if layer == 1:
                dve.wait_ge(ranked, 1)
                link(v.tensor_scalar(over, te(RANK[:, :]), float(CAP1), float(OUT_OF_RANGE), ALU.is_ge, ALU.mult))
            dve.wait_ge(ends_done, 1)
            link(v.tensor_scalar(offset, ENDS[:, 0:EXPERTS], float(P), None, ALU.mult))
            link(v.tensor_scalar(ended, ENDS[:, 1:EXPERTS + 1], s.c("index"), None, ALU.is_le))
            link(v.tensor_reduce(tile_col, ended, AX.X, ALU.add))
            v.tensor_scalar(tile_col, tile_col, float(EXPERTS - 1), None, ALU.min).then_inc(col_ready, 1)
            dve.wait_ge(ranked, 1)
            if layer == 0:
                link(v.tensor_tensor(rd, te(RANK[:, :]), over_tiles(offset), ALU.add))
            else:
                link(v.scalar_tensor_tensor(out=rd, in0=te(RANK[:, :]), scalar=float(CAP1 - 1), in1=over_tiles(offset),
                                            op0=ALU.min, op1=ALU.add))
                link(v.tensor_tensor(rd, rd, over, ALU.add))
            for k in range(TOPK):
                ins = v.tensor_tensor(picked[k], onehot[k], rd, ALU.mult)
            link(ins)
            for k in range(TOPK):
                ins = v.tensor_reduce(slot_f[:, k * TILES:(k + 1) * TILES], picked[k], AX.X, ALU.add)
            link(ins)
            slots = slot_f.rearrange("p (k t) -> p k t", k=TOPK)
            if layer == 0:
                link(v.tensor_copy(s.slot_r[:], slots))
            else:
                link(v.tensor_copy(s.slot_w[:], slots))
                v.tensor_scalar(s.slot_r[:], s.slot_w[:], OUT_OF_RANGE - 1, None, ALU.bitwise_and).then_inc(slots_done, 1)
            dve.wait_ge(row_done, 1)
            v.tensor_copy(s.tile_expert[:], TILE_ROW[:, :]).then_inc(row_read, 1)
            if layer == 0:
                return
            for b in range(1, BATCH):
                hidden(b - 1)
                take(b)
                add_down(b - 1)
            hidden(BATCH - 1)
            add_down(BATCH - 1)


def scatter_tile(nc, s, d, layer, t, scattered, choices=range(TOPK)):
    slot = s.slot_r if layer == 0 else s.slot_w
    for k in choices:
        nc.gpsimd.indirect_dma_start(
            out=d["xs"], out_offset=bass.IndirectOffsetOnAxis(ap=slot[:, k, t:t + 1], axis=0),
            in_=s.xn[:, t, :], in_offset=None, bounds_check=SLOTS - 1, oob_is_err=False,
        ).then_inc(scattered[k], 16)



ROW_AT = [0, P, 3 * P, 6 * P]
COL_AT = [0, 4 * P, 7 * P, 9 * P]
SCORE_BANK = [(1, 384), (2, 0), (1, 0), (0, 0)]
ORDER = (3, 2, 0, 1)
BANK_FULL = {3: 1, 2: 3, 0: 3, 1: 4}
TURN_BANK = [(3, 0), (4, 0), (5, 0), (4, 384)]


def attention_block0(nc, s, d, rows, extra):
    NU = len(rows) * H0
    def parts(at, width):
        return [s.parts[:, at + i * width:at + (i + 1) * width] for i in range(2)]

    x_parts = [a.rearrange("p (b k n) -> p b k n", b=len(rows), k=KC) for a in parts(0, len(rows) * KC * SEQ)]
    w_parts = [a.rearrange("p (j k n) -> p j k n", j=2, k=KC) for a in parts(2 * len(rows) * KC * SEQ, 2 * KC * P)]
    with signals(nc, f"a{rows[0]}") as sem, ExitStack() as ctx:
        xhigh, xlow, whigh, wlow = map(sem, ("xhigh", "xlow", "whigh", "wlow"))
        q_done, rope_part, q_ready, k_ready = map(sem, ("q_done", "rope_part", "q_ready", "k_ready"))
        scored, maxed, exped, rsum_ready, prob_ready = map(sem, ("scored", "maxed", "exped", "rsum", "prob"))
        turned, out_v, out_a, weighted, o_ready = map(sem, ("turned", "outv", "outa", "weighted", "o_ready"))
        wout_done, x_added = map(sem, ("wout_done", "x_added"))
        w_in = [sem(f"wq_in{i}") for i in range(2)]
        kh_in = [sem(f"kh_in{i}") for i in range(2)]
        gathered = [sem(f"gathered{i}") for i in range(UNROLL)]
        gu_in, stat, aggr = map(sem, ("gu_in", "stat", "aggr"))
        block = ctx.enter_context(nc.Block())

        def heads(eng, step, between, drain):
            for bi in range(len(rows)):
                step(bi * H0, bi, 0, 0)
                if bi:
                    between(bi - 1)
                step(bi * H0 + 1, bi, 1, 1)
                with eng.Fori(1, H0 // 2 - 2) as r:
                    for par in range(2):
                        step(bi * H0 + 2 * r + par, bi, 2 * r + par, par)
                for h in range(H0 - 4, H0):
                    step(bi * H0 + h, bi, h, h % 2)
            drain()
            between(len(rows) - 1)

        def next_row(bi, h):
            if isinstance(h, int) and h >= H0 - 2:
                return bi + 1 if bi + 1 < len(rows) else None
            return bi

        def loads(u, par):
            return 8 * (u - par) + 16

        combining = extra == "combine"

        def adds_before(bi, h):
            n = ROWS * bi if not (isinstance(h, int) and h == 0) else ROWS * max(bi - 1, 0)
            return n + (2 * (bi * H0 + h) if combining and bi < 2 else (2 * 2 * H0 if combining else 0))

        def wout_count(bi, i):
            if not combining:
                done = 0
            else:
                done = min(2 * ((bi + 1) * H0 + 1), 4 * H0) if bi + 1 < len(rows) else 4 * H0
                done = min(done, 4 * H0)
            return ROWS * bi + done + i + 1

        def choice_added(t, bi, k):
            h = 2 * (t - 8 * bi) + k // 2
            return adds_before(bi, h) + k % 2 + 1

        @block.sync
        def _(sp):
            def load(u, bi, h, par):
                if not (isinstance(u, int) and u < 2):
                    sp.wait_ge(wlow, u - 1)
                sp.dma_start(s.wq[:, par], d["wq0"].rearrange("(h k p) n -> p h k n", k=KC, p=P)[:, bass.ds(h, 1)].rearrange(
                    "p a k n -> p (a k) n")).then_inc(w_in[par], 16)
                if not (isinstance(u, int) and u < 2):
                    sp.wait_ge(k_ready, u - 1)
                b = rows[bi]
                sp.dma_start(s.khb[:, par], d["khT"][bass.ds(h, 1), b * SEQ:(b + 1) * SEQ].to_broadcast([P, SEQ])
                             ).then_inc(kh_in[par], 16)

            heads(sp, load, lambda _: None, lambda: None)
            if extra == "scatter":
                sp.wait_ge(q_done, NU)
                sp.dma_start(s.gu0, d["gu0"].rearrange("(k p) n -> p k n", p=P)).then_inc(gu_in, 16)
                sp.wait_ge(gu_in, 16)

        @block.gpsimd
        def _(pool):
            def split_low(u):
                par = u % 2
                pool.wait_ge(whigh, u + 1)
                if u >= 2:
                    pool.wait_ge(q_done, u - 1)
                nc.gpsimd.tensor_tensor(w_parts[1][:, par], s.wq[:, par], w_parts[0][:, par].bitcast(F32),
                                        ALU.subtract).then_inc(wlow, 1)

            def operands(u, bi, par):
                pool.wait_ge(kh_in[par], loads(u, par))
                if not (isinstance(u, int) and u < 2):
                    pool.wait_ge(scored, ROWS * (u - 1))
                b = rows[bi]
                nc.gpsimd.tensor_tensor(s.kT[:, par], s.kpT[:, b * SEQ:(b + 1) * SEQ], s.khb[:, par],
                                        ALU.mult).then_inc(k_ready, 1)
                if 1 <= u < NU - 1:
                    split_low(u + 1)
                pool.wait_ge(rope_part, u + 1)
                nc.gpsimd.tensor_tensor(s.qT[:, par], s.rope_a, s.rope_b, ALU.add).then_inc(q_ready, 1)

            split_low(0)
            split_low(1)
            for u in range(NU):
                operands(u, u // H0, u % 2)
                if extra == "scatter":
                    scatter_tile(nc, s, d, 0, u // 2, gathered, range(2 * (u % 2), 2 * (u % 2) + 2))
                else:
                    t = u // 2
                    for k in (2 * (u % 2), 2 * (u % 2) + 1):
                        if t:
                            pool.wait_ge(x_added, choice_added(t - 1, (t - 1) // 8, k))
                        nc.gpsimd.indirect_dma_start(
                            out=s.gath[0][:, k], out_offset=None, in_=d["ys"],
                            in_offset=bass.IndirectOffsetOnAxis(ap=s.slot_r[:, k, t:t + 1], axis=0),
                        ).then_inc(gathered[k], 16)
            if extra == "scatter":
                for k in range(TOPK):
                    pool.wait_ge(gathered[k], 16 * TILES)

        @block.tensor
        def _(pe):
            def query(u, bi, par):
                pe.wait_ge(whigh, u + 1)
                pe.wait_ge(wlow, u + 1)
                pe.wait_ge(xhigh, bi + 1)
                pe.wait_ge(xlow, bi + 1)
                if not (isinstance(u, int) and u == 0):
                    pe.wait_ge(rope_part, u)
                n = 0
                for k in range(KC):
                    for wp, xp in ((0, 0), (0, 1), (1, 0)):
                        mm = nc.tensor.matmul(s.ps[6][:, :], w_parts[wp][:, par, k, :],
                                              x_parts[xp][:, bi, k, :], start=n == 0, stop=n == 3 * KC - 1)
                        n += 1
                mm.then_inc(q_done, 1)

            def scores(u, par):
                pe.wait_ge(q_ready, u + 1)
                pe.wait_ge(k_ready, u + 1)
                if not (isinstance(u, int) and u == 0):
                    pe.wait_ge(exped, ROWS * u)
                for i in ORDER:
                    bank, at = SCORE_BANK[i]
                    w = (i + 1) * P
                    nc.tensor.matmul(s.ps[bank][:, at:at + w], s.qT[:, par, i * P:(i + 1) * P], s.kT[:, par, 0:w],
                                     start=True, stop=False)
                    nc.tensor.matmul(s.ps[bank][:, at + w - P:at + w], s.identb[:], s.maskb[:],
                                     start=False, stop=True).then_inc(scored, 1)

            def turn(u, par):
                pe.wait_ge(prob_ready, ROWS * u + ROWS)
                if not (isinstance(u, int) and u == 0):
                    pe.wait_ge(out_v, u)
                    pe.wait_ge(out_a, (ROWS - 1) * u)
                for j in (0, 1, 3, 2):
                    bank, at = TURN_BANK[j]
                    for i in range(j, ROWS):
                        mm = nc.tensor.transpose(s.ps[bank][:, at + (i - j) * P:at + (i - j + 1) * P],
                                                 s.probs[:, par, ROW_AT[i] + j * P:ROW_AT[i] + (j + 1) * P], s.c("ident"))
                    mm.then_inc(turned, 1)

            def values(u, bi):
                if not (isinstance(u, int) and u == 0):
                    pe.wait_ge(o_ready, u)
                pe.wait_ge(out_v, u + 1)
                pe.wait_ge(out_a, (ROWS - 1) * (u + 1))
                for j in range(ROWS):
                    w = (ROWS - j) * P
                    mm = nc.tensor.matmul(s.ps[7][:, j * P:], s.vp[:, rows[bi] * ROWS + j, :],
                                          s.probsT[:, COL_AT[j]:COL_AT[j] + w], start=j == 0, stop=j == ROWS - 1)
                mm.then_inc(weighted, 1)

            def step(u, bi, h, par):
                scores(u, par)
                first = isinstance(u, int) and u == 0
                if isinstance(h, int) and h == 1 and bi:
                    pe.wait_ge(x_added, wout_count(bi - 1, ROWS - 1))
                if not first:
                    turn(u - 1, 1 - par)
                ahead = next_row(bi, h)
                if ahead is not None:
                    query(u + 2, ahead, par)
                if not first:
                    values(u - 1, bi - 1 if isinstance(h, int) and h == 0 else bi)

            def project(bi):
                pe.wait_ge(o_ready, H0 * (bi + 1))
                for i in range(ROWS):
                    bank = 3 + i % 2
                    if i >= 2:
                        pe.wait_ge(x_added, wout_count(bi, i - 2))
                    else:
                        pe.wait_ge(out_v, H0 * (bi + 1))
                        pe.wait_ge(out_a, (ROWS - 1) * H0 * (bi + 1))
                    for h in range(H0):
                        mm = nc.tensor.matmul(s.ps[bank][:, 0:EMB], s.oT[:, h, i * P:(i + 1) * P], s.wout[:, h, :],
                                              start=h == 0, stop=h == H0 - 1)
                    mm.then_inc(wout_done, 1)

            def drain():
                u = NU - 1
                turn(u, 1)
                values(u, len(rows) - 1)

            query(0, 0, 0)
            query(1, 0, 1)
            heads(pe, step, project, drain)

        @block.vector
        def _(dve):
            v = nc.vector

            def x_low(bi):
                dve.wait_ge(xhigh, bi + 1)
                b = rows[bi]
                v.tensor_tensor(x_parts[1][:, bi], s.xnT[:, :, b * SEQ:(b + 1) * SEQ], x_parts[0][:, bi].bitcast(F32),
                                ALU.subtract).then_inc(xlow, 1)

            def rotate(u, par):
                dve.wait_ge(q_done, u + 1)
                if not (isinstance(u, int) and u == 0):
                    dve.wait_ge(q_ready, u)
                rope0(nc, s, s.ps[6]).then_inc(rope_part, 1)

            def maxima(u, par):
                for n, i in enumerate(ORDER):
                    bank, at = SCORE_BANK[i]
                    dve.wait_ge(scored, ROWS * u + BANK_FULL[i])
                    if n == 0 and not (isinstance(u, int) and u < 2):
                        dve.wait_ge(exped, ROWS * (u - 1))
                    v.tensor_reduce(s.negmax[:, par, i:i + 1], s.ps[bank][:, at:at + (i + 1) * P], AX.X, ALU.max,
                                    negate=True).then_inc(maxed, 1)

            def normalise(u, par):
                dve.wait_ge(exped, ROWS * (u + 1))
                if not (isinstance(u, int) and u < 2):
                    dve.wait_ge(prob_ready, ROWS * (u - 1))
                v.reciprocal(s.rsum[:, par], s.psumrow[:, par]).then_inc(rsum_ready, 1)
                dve.wait_ge(rsum_ready, u + 1)
                for i in reversed(range(ROWS)):
                    row = s.probs[:, par, ROW_AT[i]:ROW_AT[i] + (i + 1) * P]
                    v.tensor_scalar(row, row, s.rsum[:, par, i:i + 1], None, ALU.mult).then_inc(prob_ready, 1)

            def out0(u, bi, h):
                dve.wait_ge(turned, ROWS * u + 1)
                if not (isinstance(u, int) and u == 0):
                    dve.wait_ge(weighted, u)
                bank, at = TURN_BANK[0]
                v.tensor_scalar(s.probsT[:, COL_AT[0]:COL_AT[0] + SEQ], s.ps[bank][:, 0:SEQ],
                                s.kh[:, rows[bi] * ROWS, bass.ds(H0 + h, 1)], None, ALU.mult).then_inc(out_v, 1)

            def combine(u, bi, h, par):
                n = adds_before(bi, h)
                for kk in range(2):
                    k = 2 * par + kk
                    t = 8 * bi + (h // 2 if isinstance(h, int) else (h - par) // 2)
                    dve.wait_ge(gathered[k], 16 * (t + 1))
                    if not (isinstance(n, int) and n == 0 and kk == 0):
                        dve.wait_ge(x_added, n + kk)
                    xt = s.x[:, bass.ds(t, 1), :].rearrange("p a e -> p (a e)")
                    v.scalar_tensor_tensor(out=xt, in0=s.gath[0][:, k], scalar=s.weight[:, bass.ds(t, 1), k],
                                           in1=xt, op0=ALU.mult, op1=ALU.add).then_inc(x_added, 1)

            def step(u, bi, h, par):
                maxima(u, par)
                if not (isinstance(u, int) and u == 0):
                    if isinstance(h, int) and h == 0:
                        out0(u - 1, bi - 1, H0 - 1)
                    else:
                        out0(u - 1, bi, h - 1)
                if combining and bi < 2:
                    combine(u, bi, h, par)
                if next_row(bi, h) is not None:
                    rotate(u + 2, par)
                normalise(u, par)
                if isinstance(u, int) and 1 <= u < len(rows):
                    x_low(u)

            def statistics(tiles):
                for t in tiles:
                    v.bn_stats(s.stats[:, t, :], s.x[:, t, :]).then_inc(stat, 1)

            def project(bi):
                last = combining and bi == len(rows) - 1
                if last:
                    dve.wait_ge(x_added, wout_count(bi, 0) - 1)
                    statistics(range(TILES - ROWS))
                for i in range(ROWS):
                    t = rows[bi] * ROWS + i
                    dve.wait_ge(wout_done, ROWS * bi + i + 1)
                    if wout_count(bi, i) > 1:
                        dve.wait_ge(x_added, wout_count(bi, i) - 1)
                    v.tensor_tensor(s.x[:, t, :], s.ps[3 + i % 2][:, 0:EMB], s.x[:, t, :], ALU.add).then_inc(x_added, 1)
                    if last and i:
                        dve.wait_ge(x_added, wout_count(bi, i - 1))
                        statistics([t - 1])
                if last:
                    dve.wait_ge(x_added, wout_count(bi, ROWS - 1))
                    statistics([TILES - 1])
                    for t in range(TILES):
                        dve.wait_ge(stat, t + 1)
                        v.bn_aggr(s.meanvar[:, t, :], s.stats[:, t, :]).then_inc(aggr, 1)

            x_low(0)
            rotate(0, 0)
            rotate(1, 1)
            heads(dve, step, project, lambda: out0(NU - 1, len(rows) - 1, H0 - 1))

        @block.scalar
        def _(act):
            def x_high(bi):
                b = rows[bi]
                nc.scalar.activation(x_parts[0][:, bi], s.xnT[:, :, b * SEQ:(b + 1) * SEQ],
                                     ACT.Copy).then_inc(xhigh, 1)

            def split_high(u, par):
                act.wait_ge(w_in[par], loads(u, par))
                if not (isinstance(u, int) and u < 2):
                    act.wait_ge(q_done, u - 1)
                nc.scalar.activation(w_parts[0][:, par], s.wq[:, par], ACT.Copy).then_inc(whigh, 1)

            def exps(u, par, which):
                for n, i in list(enumerate(ORDER))[which]:
                    bank, at = SCORE_BANK[i]
                    act.wait_ge(maxed, ROWS * u + BANK_FULL[i])
                    if n == 0 and not (isinstance(u, int) and u < 2):
                        act.wait_ge(turned, ROWS * (u - 1))
                    nc.scalar.activation(s.probs[:, par, ROW_AT[i]:ROW_AT[i] + (i + 1) * P],
                                         s.ps[bank][:, at:at + (i + 1) * P], ACT.Exp,
                                         bias=s.negmax[:, par, i:i + 1],
                                         accum_out=s.psumrow[:, par, i:i + 1]).then_inc(exped, 1)

            def outs(u, bi, h):
                if not (isinstance(u, int) and u == 0):
                    act.wait_ge(weighted, u)
                for n, j in enumerate((1, 3, 2)):
                    bank, at = TURN_BANK[j]
                    w = (ROWS - j) * P
                    act.wait_ge(turned, ROWS * u + (3 if n < 2 else 4))
                    nc.scalar.activation(s.probsT[:, COL_AT[j]:COL_AT[j] + w], s.ps[bank][:, at:at + w], ACT.Copy,
                                         scale=s.kh[:, rows[bi] * ROWS + j, bass.ds(H0 + h, 1)]).then_inc(out_a, 1)

            def heads_out(u, bi, h):
                act.wait_ge(weighted, u + 1)
                if bi > 0 and isinstance(h, int) and h == 0:
                    act.wait_ge(wout_done, ROWS * bi)
                nc.scalar.activation(s.oT[:, bass.ds(h, 1)].rearrange("p a n -> p (a n)"), s.ps[7][:, :],
                                     ACT.Copy).then_inc(o_ready, 1)

            def step(u, bi, h, par):
                before = (bi - 1, H0 - 1) if isinstance(h, int) and h == 0 else (bi, h - 1)
                first = isinstance(u, int) and u == 0
                exps(u, par, slice(0, 2))
                if not first:
                    outs(u - 1, *before)
                exps(u, par, slice(2, 4))
                if not first:
                    heads_out(u - 1, *before)
                if not (isinstance(u, int) and u + 3 >= NU):
                    split_high(u + 3, 1 - par)

            def drain():
                outs(NU - 1, len(rows) - 1, H0 - 1)
                heads_out(NU - 1, len(rows) - 1, H0 - 1)

            x_high(0)
            split_high(0, 0)
            split_high(1, 1)
            for bi in range(1, len(rows)):
                x_high(bi)
            split_high(2, 0)
            heads(act, step, lambda _: None, drain)




def expert_block(nc, s, d, layer):
    inter = I0 if layer == 0 else I1
    gu, dn = (s.gu0, s.dn0) if layer == 0 else (s.gu1, s.dn1)
    W = 2 * inter
    rows_in = s.probs[:].rearrange("p a n -> p (a n)")[:, 0:UNROLL * EMB].rearrange("p (j e) -> p j e", j=UNROLL)
    rowsT = s.probsT[:, 0:2 * EMB].rearrange("p (j n) -> p j n", j=2)
    outs = s.rope.rearrange("p a (b e) -> p (a b) e", e=EMB)
    silu, hid, hidT = (s.khb.rearrange("p a n -> p (a n)")[:, 2 * P * i:2 * P * (i + 1)].rearrange("p (j n) -> p j n", j=2)
                       for i in range(3))
    silu, hid = silu[:, :, 0:inter], hid[:, :, 0:inter]
    with signals(nc, f"e{layer}") as sem, ExitStack() as ctx:
        turned, rowsT_ready, gu_done, silu_done, hid_ready, hid_turned, hidT_ready, down_done, out_ready = map(
            sem, ("turned", "rowsT", "gu_done", "silu", "hid", "hid_turned", "hidT", "down", "out"))
        w_in = sem("w_in")
        x_in = [sem(f"x_in{j}") for j in range(UNROLL)]
        y_out = [sem(f"y_out{j}") for j in range(UNROLL)]
        block = ctx.enter_context(nc.Block())
        N = SLOT_TILES

        def known(i):
            return isinstance(i, int)

        def tiles(eng, step, tail):
            for i in range(UNROLL):
                step(i, i)
            with eng.Fori(0, (N - 2 * UNROLL) // STEPS) as r:
                for j in range(STEPS):
                    step(STEPS * r + (UNROLL + j), (UNROLL + j) % STEPS)
            for i in range(N - UNROLL, N + tail):
                step(i, i % STEPS)

        @block.sync
        def _(sp):
            def load(i, j):
                if layer == 0 and known(i) and i == 2:
                    sp.dma_start(dn, d["dn0"]).then_inc(w_in, 16)
                j %= UNROLL
                if not (known(i) and i < UNROLL):
                    sp.wait_ge(turned, i - UNROLL + 1)
                sp.dma_start(rows_in[:, j], d["xs"][bass.ds(i * P, P), :]).then_inc(x_in[j], 16)

            tiles(sp, load, 0)
            if layer == 0:
                sp.wait_ge(w_in, 16)

        @block.tensor
        def _(pe):
            def turn_rows(i, j):
                pe.wait_ge(x_in[j], 4 * (i - j) + 16)
                if not (known(i) and i < 2):
                    pe.wait_ge(rowsT_ready, i - 1)
                for k in range(KC):
                    mm = nc.tensor.transpose(s.ps[j % 2][:, k * P:(k + 1) * P], rows_in[:, j, k * P:(k + 1) * P],
                                             s.c("ident"))
                mm.then_inc(turned, 1)

            expert = [pe.alloc_register(f"expert{j}_e{layer}") for j in range(STEPS)]

            def read_expert(i, j):
                pe.reg_load(expert[j], s.tile_expert[0:1, bass.ds(i, 1)])

            def gate_up(i, j):
                e = pe.snap(expert[j], min_val=0, max_val=EXPERTS - 1)
                pe.wait_ge(rowsT_ready, i + 1)
                if not (known(i) and i < 2):
                    pe.wait_ge(hid_ready, i - 1)
                for k in range(KC):
                    mm = nc.tensor.matmul(s.ps[2 + j % 2][:, 0:W], rowsT[:, j % 2, k * P:(k + 1) * P],
                                          gu[:, k, bass.ds(e * W, W)], start=k == 0, stop=k == KC - 1)
                mm.then_inc(gu_done, 1)

            def turn_hidden(i, j):
                pe.wait_ge(hid_ready, i + 1)
                if not (known(i) and i < 2):
                    pe.wait_ge(hidT_ready, i - 1)
                nc.tensor.transpose(s.ps[4 + j % 2][0:inter, 0:P], hid[:, j % 2, :], s.c("ident")).then_inc(hid_turned, 1)

            def down(i, j):
                e = pe.snap(expert[j], min_val=0, max_val=EXPERTS - 1)
                if layer == 0 and known(i) and i == 0:
                    pe.wait_ge(w_in, 16)
                pe.wait_ge(hidT_ready, i + 1)
                if not (known(i) and i < 2):
                    pe.wait_ge(out_ready, i - 1)
                nc.tensor.matmul(s.ps[6 + j % 2][:, 0:EMB], hidT[0:inter, j % 2, :], dn[0:inter, bass.ds(e * EMB, EMB)],
                                 start=True, stop=True).then_inc(down_done, 1)

            def step(i, j):
                if not known(i) or i < N:
                    gate_up(i, j)
                if not known(i) or i + 2 < N:
                    read_expert(i + 2, (j + 2) % STEPS)
                    turn_rows(i + 2, (j + 2) % UNROLL)
                if not known(i) or 1 <= i < N + 1:
                    turn_hidden(i - 1, (j - 1) % UNROLL)
                if not known(i) or 2 <= i < N + 2:
                    down(i - 2, (j - 2) % STEPS)

            read_expert(0, 0)
            read_expert(1, 1)
            turn_rows(0, 0)
            turn_rows(1, 1)
            tiles(pe, step, 2)

        @block.scalar
        def _(act):
            def gate(i, j):
                act.wait_ge(gu_done, i + 1)
                if not (known(i) and i < 2):
                    act.wait_ge(hid_ready, i - 1)
                nc.scalar.activation(silu[:, j % 2, :], s.ps[2 + j % 2][:, 0:inter], ACT.Silu).then_inc(silu_done, 1)

            def out(i, j):
                j %= UNROLL
                act.wait_ge(down_done, i + 1)
                if not (known(i) and i < UNROLL):
                    act.wait_ge(y_out[j], 4 * (i - j))
                nc.scalar.activation(outs[:, j], s.ps[6 + j % 2][:, 0:EMB], ACT.Copy).then_inc(out_ready, 1)
                act.wait_ge(out_ready, i + 1)
                act.dma_start(d["ys"][bass.ds(i * P, P), :], outs[:, j]).then_inc(y_out[j], 16)

            def step(i, j):
                if not known(i) or i < N:
                    gate(i, j)
                if not known(i) or 2 <= i < N + 2:
                    out(i - 2, (j - 2) % UNROLL)

            tiles(act, step, 2)
            for j in range(UNROLL):
                act.wait_ge(y_out[j], 16 * N // UNROLL)

        @block.vector
        def _(dve):
            v = nc.vector

            def rowsT_out(i, j):
                dve.wait_ge(turned, i + 1)
                if not (known(i) and i < 2):
                    dve.wait_ge(gu_done, i - 1)
                v.tensor_copy(rowsT[:, j % 2, :], s.ps[j % 2][:, 0:EMB]).then_inc(rowsT_ready, 1)

            def hidden(i, j):
                dve.wait_ge(silu_done, i + 1)
                if not (known(i) and i < 2):
                    dve.wait_ge(hid_turned, i - 1)
                v.tensor_tensor(hid[:, j % 2, :], silu[:, j % 2, :], s.ps[2 + j % 2][:, inter:W], ALU.mult).then_inc(hid_ready, 1)

            def hidT_out(i, j):
                dve.wait_ge(hid_turned, i + 1)
                if not (known(i) and i < 2):
                    dve.wait_ge(down_done, i - 1)
                v.tensor_copy(hidT[0:inter, j % 2, :], s.ps[4 + j % 2][0:inter, 0:P]).then_inc(hidT_ready, 1)

            def step(i, j):
                if not known(i) or i + 2 < N:
                    rowsT_out(i + 2, (j + 2) % UNROLL)
                if not known(i) or i < N:
                    hidden(i, j)
                if not known(i) or 1 <= i < N + 1:
                    hidT_out(i - 1, (j - 1) % UNROLL)

            rowsT_out(0, 0)
            rowsT_out(1, 1)
            tiles(dve, step, 2)




def values1(s):
    return [a.rearrange("p (i n) -> p i n", i=ROWS) for a in (s.qT[:, 0], s.qT[:, 1], s.kT[:, 0], s.kT[:, 1])]


def norm_block1(nc, s, d):
    xn1 = s.big_a[:, 0:TILES * EMB].rearrange("p (t e) -> p t e", t=TILES)
    xfT = s.big_b[:, 0:KC * TOKENS].rearrange("p (k n) -> p k n", k=KC)
    nw, gate, sg, su, sd = shared_weights(s)
    rms = s.kh[:, 0, 0:TILES]
    wqs, bqs, bq = (attn1_view(s, a) for a in ("wqs", "bqs", "bq"))
    wqs = wqs.rearrange("p (k n) -> p k n", k=KC)
    raw_q = attn1_view(s, "raw_q").rearrange("p (k g n) -> p k g n", k=KC, g=GROUPS1)
    with signals(nc, "n1") as sem, ExitStack() as ctx:
        w_in, attn_in, var_ready, std_ready, rstd_ready, xn_ready = map(
            sem, ("w_in", "attn_in", "var", "std", "rstd", "xn"))
        dlink, ms_ready, rms_std, rms_ready, xf_ready, plink = map(
            sem, ("dlink", "ms", "rms_std", "rms", "xf", "plink"))
        turned_n, xnT_ready, turned_f, xfT_ready, logits_done, logits_out = map(
            sem, ("turned_n", "xnT", "turned_f", "xfT", "logits_done", "logits_out"))
        block = ctx.enter_context(nc.Block())

        @block.sync
        def _(sp):
            def kchunks(a):
                return a.rearrange("(k p) n -> p k n", p=P)

            def load(name, src, k=None):
                dst = attn1_view(s, name)
                sp.dma_start(dst if k is None else dst.rearrange("p (k n) -> p k n", k=k), src).then_inc(attn_in, 16)

            load("raw_q", kchunks(d["wq1"]), KC)
            load("bq", d["bq"])
            sp.dma_start(nw, d["normw1"].to_broadcast([P, EMB])).then_inc(w_in, 16)
            sp.dma_start(gate, kchunks(d["gate1"])).then_inc(w_in, 16)
            sp.dma_start(sg, kchunks(d["sg1"])).then_inc(w_in, 16)
            sp.dma_start(su, kchunks(d["su1"])).then_inc(w_in, 16)
            sp.dma_start(sd, d["sd1"]).then_inc(w_in, 16)
            for name in ("wka", "wkb", "wv"):
                load(name, kchunks(d[name]), KC)
            load("rotate", d["rotate1"])
            load("wo", d["wo1"])
            load("bv", d["bv1"].to_broadcast([P, P]))
            load("bka", d["bka"])
            load("bkb", d["bkb"])
            sp.wait_ge(w_in, 16 * 5)
            sp.wait_ge(attn_in, 16 * 10)

        @block.gpsimd
        def _(pool):
            add = nc.gpsimd.tensor_tensor
            link = Link(pool, plink)
            pool.wait_ge(attn_in, 16 * 10)
            link(add(wqs, raw_q[:, :, 0], raw_q[:, :, 1], ALU.add))
            link(add(wqs, wqs, raw_q[:, :, 2], ALU.add))
            link(add(wqs, wqs, raw_q[:, :, 3], ALU.add))
            link(add(bqs, bq[:, 0:1], bq[:, 1:2], ALU.add))
            link(add(bqs, bqs, bq[:, 2:3], ALU.add))
            link(add(bqs, bqs, bq[:, 3:4], ALU.add))
            for c in range(4):
                pool.wait_ge(xn_ready, 4 * c + 4)
                tiles = slice(4 * c, 4 * c + 4)
                link(add(s.x[:, tiles], s.x[:, tiles], xn1[:, tiles], ALU.add))

        @block.vector
        def _(dve):
            v = nc.vector
            link = Link(dve, dlink)
            v.tensor_scalar(s.rstd[:], s.meanvar[:, :, 1], 1e-5, None, ALU.add).then_inc(var_ready, 1)
            dve.wait_ge(std_ready, 1)
            v.reciprocal(s.rstd[:], s.rstd[:]).then_inc(rstd_ready, 1)
            dve.wait_ge(rstd_ready, 1)
            link(v.tensor_tensor(rms, s.meanvar[:, :, 1], s.rstd[:], ALU.mult))
            link(v.tensor_tensor(rms, rms, s.rstd[:], ALU.mult))
            v.tensor_scalar(rms, rms, 1e-6, None, ALU.add).then_inc(ms_ready, 1)
            for t in range(TILES):
                v.tensor_scalar(xn1[:, t, :], s.x[:, t, :], s.meanvar[:, t, 0:1], s.rstd[:, t:t + 1],
                                ALU.subtract, ALU.mult).then_inc(xn_ready, 1)
            dve.wait_ge(rms_std, 1)
            v.reciprocal(rms, rms).then_inc(rms_ready, 1)
            dve.wait_ge(rms_ready, 1)
            dve.wait_ge(w_in, 16 * 5)
            for t in range(TILES):
                dve.wait_ge(xn_ready, t + 1)
                v.scalar_tensor_tensor(out=s.xn[:, t, :], in0=xn1[:, t, :], scalar=rms[:, t:t + 1], in1=nw,
                                       op0=ALU.mult, op1=ALU.mult).then_inc(xf_ready, 1)
            dve.wait_ge(logits_done, 1)
            v.tensor_copy(s.logits[:], s.ps[7][:, :].rearrange("p (t e) -> p t e", t=TILES)).then_inc(logits_out, 1)

        @block.scalar
        def _(act):
            a = nc.scalar.activation
            act.wait_ge(var_ready, 1)
            a(s.rstd[:], s.rstd[:], ACT.Sqrt).then_inc(std_ready, 1)
            act.wait_ge(ms_ready, 1)
            a(rms, rms, ACT.Sqrt).then_inc(rms_std, 1)
            for dst, turned, out in ((s.xnT, turned_n, xnT_ready), (xfT, turned_f, xfT_ready)):
                for g in range(TILES // 4 * KC):
                    act.wait_ge(turned, g + 1)
                    a(dst[:, g % KC, g // KC * 512:(g // KC + 1) * 512], s.ps[g % 4][:, :], ACT.Copy).then_inc(out, 1)

        @block.tensor
        def _(pe):
            def logits(c):
                pe.wait_ge(w_in, 16 * 5)
                pe.wait_ge(xfT_ready, KC * (c + 1))
                for t in range(4 * c, 4 * c + 4):
                    for k in range(KC):
                        mm = nc.tensor.matmul(s.ps[7][:, t * EXPERTS:(t + 1) * EXPERTS], xfT[:, k, t * P:(t + 1) * P],
                                              gate[:, k, :], start=k == 0, stop=k == KC - 1)
                return mm

            groups = TILES // 4 * KC
            for src, ready, turned, taken, before in ((xn1, xn_ready, turned_n, xnT_ready, None),
                                                      (s.xn, xf_ready, turned_f, xfT_ready, xnT_ready)):
                for g in range(groups):
                    c, k = g // KC, g % KC
                    pe.wait_ge(ready, 4 * c + 4)
                    if g >= 4:
                        pe.wait_ge(taken, g - 3)
                    elif before is not None:
                        pe.wait_ge(before, groups - 3 + g)
                    for i in range(4):
                        mm = nc.tensor.transpose(s.ps[g % 4][:, i * P:(i + 1) * P],
                                                 src[:, 4 * c + i, k * P:(k + 1) * P], s.c("ident"))
                    mm.then_inc(turned, 1)
                    if src is s.xn and k == KC - 1 and c:
                        logits(c - 1)
            logits(TILES // 4 - 1).then_inc(logits_done, 1)




def attention_block1(nc, s, d, rows, extra):
    NU = len(rows) * H1
    wo = attn1_view(s, "wo")
    queries, keys, values = s.xnT[:, 0], s.xnT[:, 1], values1(s)
    headsT = s.wq[:].rearrange("p a k n -> p (a k n)")
    gath = s.big_a[:, 0:TILES * TOPK * EMB].rearrange("p (j e) -> p j e", j=TILES * TOPK)
    probsT = (s.probsT, s.work)
    scattering = extra == "scatter"
    with signals(nc, f"c{rows[0]}") as sem, ExitStack() as ctx:
        scored, maxed, exped, rsum_ready, prob_ready = map(sem, ("scored", "maxed", "exped", "rsum", "prob"))
        turned, out_v, out_a, weighted, heads_ready, wo_done, x_added = map(
            sem, ("turned", "outv", "outa", "weighted", "heads", "wo_done", "x_added"))
        moved = [sem(f"moved{i}") for i in range(TOPK)]
        gathered = [] if scattering else [sem(f"gathered{t}") for t in range(TILES)]
        w_in, y_stored = sem("w_in"), sem("y_stored")
        block = ctx.enter_context(nc.Block())

        PER_UNIT, LAST = 7, 8
        EARLY = 0 if scattering else 1
        order = []
        left = [] if scattering else [("row", t + i, k) for t in range(0, TILES, 2) for k in range(TOPK) for i in range(2)]
        for u in range(NU):
            n = min(len(left), PER_UNIT) if u else 0
            order.append((u, left[:n]))
            left = left[n:]
            bi, half = divmod(u - 2 - H1, H1)
            if bi >= 0 and half < 2:
                order[-1][1].append(("wo", bi, half))
        split = max(0, len(left) - LAST)
        order.append((NU, left[:split] + [("wo", len(rows) - 1, half) for half in range(2)] + left[split:]))
        flat = [x for _, xs in order for x in xs]
        count_of = {x: n + 1 for n, x in enumerate(flat)}

        def out_bank(bi, half):
            return s.ps[0] if half and bi == len(rows) - 1 else s.ps[6]

        @block.sync
        def _(sp):
            if scattering:
                sp.dma_start(s.gu1, d["gu1"].rearrange("(k p) n -> p k n", p=P)).then_inc(w_in, 16)
                sp.dma_start(s.dn1, d["dn1"]).then_inc(w_in, 16)
                sp.wait_ge(w_in, 32)
            else:
                out = d["out"].rearrange("(t p) e -> p t e", p=P)
                for g in range(TILES // 2):
                    last = [count_of["row", t, k] for t in (2 * g, 2 * g + 1) for k in range(TOPK)]
                    b, i = 2 * g // ROWS, 2 * g % ROWS
                    if b in rows:
                        last.append(count_of["wo", rows.index(b), i // 2])
                    sp.wait_ge(x_added, max(last))
                    sp.dma_start(out[:, 2 * g:2 * g + 2], s.x[:, 2 * g:2 * g + 2]).then_inc(y_stored, 16)
                sp.wait_ge(y_stored, 16 * TILES // 2)

        @block.gpsimd
        def _(pool):
            if scattering:
                for t in range(EARLY_TILES, TILES):
                    scatter_tile(nc, s, d, 1, t, moved)
                for k in range(TOPK):
                    pool.wait_ge(moved[k], 16 * (TILES - EARLY_TILES))
            else:
                for t in range(TILES):
                    for k in range(TOPK):
                        nc.gpsimd.indirect_dma_start(
                            out=gath[:, t * TOPK + k], out_offset=None, in_=d["ys"],
                            in_offset=bass.IndirectOffsetOnAxis(ap=s.slot_r[:, k, t:t + 1], axis=0),
                        ).then_inc(gathered[t], 16)

        @block.tensor
        def _(pe):
            def scores(u):
                bi, h = divmod(u, H1)
                if u:
                    pe.wait_ge(exped, ROWS * u)
                lanes, at0 = slice(h * HP1, (h + 1) * HP1), rows[bi] * SEQ
                for i in ORDER:
                    bank, at = SCORE_BANK[i]
                    w = (i + 1) * P
                    nc.tensor.matmul(s.ps[bank][:, at:at + w], queries[lanes, at0 + i * P:at0 + (i + 1) * P],
                                     keys[lanes, at0:at0 + w], start=True, stop=False)
                    nc.tensor.matmul(s.ps[bank][:, at + w - P:at + w], s.identb[:], s.maskb[:],
                                     start=False, stop=True).then_inc(scored, 1)

            def turn(u):
                pe.wait_ge(prob_ready, ROWS * u + ROWS)
                if u:
                    pe.wait_ge(out_v, u)
                    pe.wait_ge(out_a, (ROWS - 1) * u)
                for j in (0, 1, 3, 2):
                    bank, at = TURN_BANK[j]
                    for i in range(j, ROWS):
                        mm = nc.tensor.transpose(s.ps[bank][:, at + (i - j) * P:at + (i - j + 1) * P],
                                                 s.probs[:, u % 2, ROW_AT[i] + j * P:ROW_AT[i] + (j + 1) * P], s.c("ident"))
                    mm.then_inc(turned, 1)

            def weigh(u):
                bi, h = divmod(u, H1)
                if h == 0 and bi:
                    pe.wait_ge(heads_ready, bi)
                pe.wait_ge(out_v, u + 1)
                pe.wait_ge(out_a, (ROWS - 1) * (u + 1))
                lanes = slice(h * HP1, (h + 1) * HP1)
                for j in range(ROWS):
                    mm = nc.tensor.matmul(s.ps[7][lanes, j * P:], values[rows[bi]][:, j, lanes],
                                          probsT[u % 2][:, COL_AT[j]:COL_AT[j] + (ROWS - j) * P], start=j == 0, stop=j == ROWS - 1)
                mm.then_inc(weighted, 1)

            def out(bi, half):
                pe.wait_ge(heads_ready, bi + 1)
                if out_bank(bi, half) is s.ps[6] and (half or bi):
                    pe.wait_ge(x_added, count_of["wo", bi - 1 + half, 1 - half])
                for i in range(2):
                    t = 2 * half + i
                    mm = nc.tensor.matmul(out_bank(bi, half)[:, i * EMB:(i + 1) * EMB], headsT[:, t * P:(t + 1) * P], wo,
                                          start=True, stop=True)
                mm.then_inc(wo_done, 1)

            for u in range(NU + 2):
                if u < NU:
                    scores(u)
                if 1 <= u <= NU:
                    turn(u - 1)
                bi, half = divmod(u - 2 - H1, H1)
                if bi >= 0 and half < 2:
                    out(bi, half)
                if u >= 2:
                    weigh(u - 2)
            for half in range(2):
                out(len(rows) - 1, half)

        @block.vector
        def _(dve):
            v = nc.vector

            def maxima(u):
                for n, i in enumerate(ORDER):
                    bank, at = SCORE_BANK[i]
                    dve.wait_ge(scored, ROWS * u + BANK_FULL[i])
                    if n == 0 and u >= 2:
                        dve.wait_ge(exped, ROWS * (u - 1))
                    v.tensor_reduce(s.negmax[:, u % 2, i:i + 1], s.ps[bank][:, at:at + (i + 1) * P], AX.X, ALU.max,
                                    negate=True).then_inc(maxed, 1)

            def normalise(u):
                dve.wait_ge(exped, ROWS * (u + 1))
                if u >= 2:
                    dve.wait_ge(prob_ready, ROWS * (u - 1))
                v.reciprocal(s.rsum[:, u % 2], s.psumrow[:, u % 2]).then_inc(rsum_ready, 1)
                dve.wait_ge(rsum_ready, u + 1)
                for i in reversed(range(ROWS)):
                    row = s.probs[:, u % 2, ROW_AT[i]:ROW_AT[i] + (i + 1) * P]
                    v.tensor_scalar(row, row, s.rsum[:, u % 2, i:i + 1], None, ALU.mult).then_inc(prob_ready, 1)

            def out0(u):
                dve.wait_ge(turned, ROWS * u + 1)
                if u >= 2:
                    dve.wait_ge(weighted, u - 1)
                v.tensor_copy(probsT[u % 2][:, 0:SEQ], s.ps[TURN_BANK[0][0]][:, 0:SEQ]).then_inc(out_v, 1)

            done, last_at = [0], {}

            def additions(u, which=slice(None)):
                for at, what in order:
                    if at != u:
                        continue
                    for x in what[which]:
                        kind, a, k = x
                        touched = [a] if kind == "row" else [rows[a] * ROWS + 2 * k + i for i in range(2)]
                        before = max(last_at.get(t, 0) for t in touched)
                        if before:
                            dve.wait_ge(x_added, before)
                        if kind == "wo":
                            dve.wait_ge(wo_done, 2 * a + k + 1)
                            t = rows[a] * ROWS + 2 * k
                            ins = v.tensor_tensor(s.x[:, t:t + 2, :], s.x[:, t:t + 2, :],
                                                  out_bank(a, k)[:, :].rearrange("p (t e) -> p t e", t=2), ALU.add)
                        else:
                            dve.wait_ge(gathered[a], 16 * TOPK)
                            ins = v.scalar_tensor_tensor(out=s.x[:, a, :], in0=gath[:, a * TOPK + k],
                                                         scalar=s.weight[:, a, k:k + 1], in1=s.x[:, a, :],
                                                         op0=ALU.mult, op1=ALU.add)
                        ins.then_inc(x_added, 1)
                        done[0] += 1
                        last_at.update({t: done[0] for t in touched})

            for u in range(NU):
                maxima(u)
                if u:
                    out0(u - 1)
                additions(u, slice(0, EARLY))
                normalise(u)
                additions(u, slice(EARLY, None))
            out0(NU - 1)
            additions(NU)

        @block.scalar
        def _(act):
            def exps(u):
                for n, i in enumerate(ORDER):
                    bank, at = SCORE_BANK[i]
                    act.wait_ge(maxed, ROWS * u + BANK_FULL[i])
                    if n == 0 and u >= 2:
                        act.wait_ge(turned, ROWS * (u - 1))
                    nc.scalar.activation(s.probs[:, u % 2, ROW_AT[i]:ROW_AT[i] + (i + 1) * P],
                                         s.ps[bank][:, at:at + (i + 1) * P], ACT.Exp, bias=s.negmax[:, u % 2, i:i + 1],
                                         accum_out=s.psumrow[:, u % 2, i:i + 1]).then_inc(exped, 1)

            def outs(u):
                if u >= 2:
                    act.wait_ge(weighted, u - 1)
                for n, j in enumerate((1, 3, 2)):
                    bank, at = TURN_BANK[j]
                    w = (ROWS - j) * P
                    act.wait_ge(turned, ROWS * u + (3 if n < 2 else 4))
                    nc.scalar.activation(probsT[u % 2][:, COL_AT[j]:COL_AT[j] + w], s.ps[bank][:, at:at + w],
                                         ACT.Copy).then_inc(out_a, 1)

            def heads_out(bi):
                act.wait_ge(weighted, H1 * (bi + 1))
                if bi:
                    act.wait_ge(wo_done, 2 * bi)
                nc.scalar.activation(headsT, s.ps[7][:, :], ACT.Copy).then_inc(heads_ready, 1)

            for u in range(NU + 2):
                if u < NU:
                    exps(u)
                if 1 <= u <= NU:
                    outs(u - 1)
                if u >= 2 and (u - 2) % H1 == H1 - 1:
                    heads_out((u - 2) // H1)




def constants():
    i = np.arange(P)
    c = np.zeros((P, CONST_W), np.float32)

    def put(name, v):
        a, b = const_at(name)
        c[:, a:b] = v

    put("ident", np.eye(P))
    put("before", i[:, None] < i[None, :])
    put("upto", i[:, None] <= i[None, :])
    put("ones", 1.0)
    put("mask", np.where(i[None, :] > i[:, None], MASKED, 0.0))
    put("iota", np.arange(EXPERTS)[None, :])
    put("index", i[:, None])
    pos = np.arange(SEQ, dtype=np.float32)
    inv = (np.float32(10000.0) ** (-np.arange(0, D0, 2, dtype=np.float32) / D0)).astype(np.float32)
    ang = inv[:, None] * pos[None, :]
    put("cos0", np.tile(np.cos(ang), (2, 1)))
    put("sin0", np.concatenate([np.sin(ang), -np.sin(ang)]))
    inv1 = (1.0 / np.float32(10000.0) ** (np.arange(D1 // 2, dtype=np.float32) * 2.0 / D1)).astype(np.float32)
    ang1 = inv1[:, None] * pos[None, :]
    co, si = np.cos(ang1), np.sin(ang1)
    rotate1 = [np.tile(np.concatenate(rows), (H1, 1)) for rows in (
        [co * D1 ** -0.5, co * D1 ** -0.5, si * D1 ** -0.5, si * D1 ** -0.5], [co, co, co, -co], [-si, si, si, si])]
    return c, np.concatenate(rotate1, axis=1).astype(np.float32)


def layout(inputs):
    w = {k: np.asarray(v) for k, v in inputs.items()}
    const, rotate1 = constants()
    out = {"const": const, "rotate1": rotate1, "x": w["L0_attn_x"].reshape(TOKENS, EMB)}
    kvT = w["L0_attn_Wkv"].T
    out["wcat0"] = np.concatenate([kvT[:, D0:], w["L0_attn_Wkvh"].T, w["L0_attn_Wg"].T, w["L0_ffn_gate"]], axis=1)
    out["wk0"] = kvT[:, 0:D0]
    out["wq0"] = w["L0_attn_Wq"].T.reshape(KC, P, H0, D0).transpose(2, 0, 1, 3).reshape(H0 * KC * P, D0)
    out["wout0"] = w["L0_attn_Wout"].T
    out["gu0"] = w["L0_ffn_gate_up_proj"].transpose(1, 0, 2).reshape(EMB, EXPERTS * 2 * I0)
    out["dn0"] = w["L0_ffn_down_proj"].transpose(1, 0, 2).reshape(I0, EXPERTS * EMB)
    half = D1 // 2
    first, second = 2 * np.arange(half), 2 * np.arange(half) + 1

    def spread(a, parts):
        picked = a[..., np.concatenate(parts)]
        return picked.reshape(*picked.shape[:-2], -1)

    wq = w["L1_attn_Wq"].reshape(EMB, H1, GROUPS1, D1).transpose(0, 2, 1, 3)
    out["wq1"] = spread(wq, [first, second, first, second]).reshape(EMB, GROUPS1 * P)
    bq = w["L1_attn_bq"].reshape(H1, GROUPS1, D1).transpose(1, 0, 2)
    out["bq"] = spread(bq, [first, second, first, second]).T
    wk, bk = w["L1_attn_Wk"].reshape(EMB, H1, D1), w["L1_attn_bk"].reshape(1, H1, D1)
    for name, parts in (("ka", [first, second, second, first]), ("kb", [second, first, first, second])):
        out["w" + name] = spread(wk, parts)
        out["b" + name] = spread(bk, parts).T
    def pad(a, axis):
        width = [(0, 0)] * a.ndim
        width[axis] = (0, HP1 - D1)
        return np.pad(a, width)

    out["wv"] = pad(w["L1_attn_Wv"].reshape(EMB, H1, D1), 2).reshape(EMB, P)
    out["bv1"] = pad(w["L1_attn_bv"].reshape(1, H1, D1), 2).reshape(1, P)
    out["wo1"] = pad(w["L1_attn_Wo"].reshape(H1, D1, EMB), 1).reshape(P, EMB)
    out["bv1"][0, D1], out["wo1"][D1] = 1.0, w["L1_attn_bo"]
    out["normw1"] = w["L1_ffn_norm_w"].reshape(1, EMB)
    out["gate1"] = w["L1_ffn_gate_w"].T
    out["gu1"] = w["L1_ffn_w13"].transpose(1, 0, 2).reshape(EMB, EXPERTS * 2 * I1)
    out["dn1"] = w["L1_ffn_w2"].transpose(1, 0, 2).reshape(I1, EXPERTS * EMB)
    out["sg1"], out["su1"], out["sd1"] = (w["L1_ffn_shared_gate_w"], w["L1_ffn_shared_up_w"], w["L1_ffn_shared_down_w"])
    return {k: np.ascontiguousarray(v) for k, v in out.items()}


def program(nc, d):
    with ExitStack() as ctx:
        s = make_buffers(nc, ctx)
        with signals(nc, "xs") as sem:
            xs_zeroed = sem("xs_zeroed")
            norm_block0(nc, s, d, xs_zeroed)
            route_block(nc, s, d, 0, xs_zeroed)
        attention_block0(nc, s, d, [0, 1], "scatter")
        expert_block(nc, s, d, 0)
        attention_block0(nc, s, d, [2, 3], "combine")
        norm_block1(nc, s, d)
        route_block(nc, s, d, 1)
        attention_block1(nc, s, d, [0, 1], "scatter")
        expert_block(nc, s, d, 1)
        attention_block1(nc, s, d, [2, 3], "combine")


def kernel(**inputs):
    import concourse.bacc as bacc
    from concourse.bass_utils import run_bass_kernel_spmd

    arrays = layout(inputs)
    nc = bacc.Bacc("TRN2", target_bir_lowering=False, num_devices=1)
    d = {name: nc.dram_tensor(f"in_{name}", a.shape, mybir.dt.float32, kind="ExternalInput").ap()
         for name, a in arrays.items()}
    for name, shape in dict(khT=(H0, TOKENS), xs=(SLOTS, EMB), ys=(SLOTS, EMB)).items():
        d[name] = nc.dram_tensor(f"{name}_dram", shape, mybir.dt.float32).ap()
    d["out"] = nc.dram_tensor("out", (TOKENS, EMB), mybir.dt.float32, kind="ExternalOutput").ap()
    program(nc, d)
    result = run_bass_kernel_spmd(nc, [{f"in_{name}": a for name, a in arrays.items()}], core_ids=[0])
    return result.results[0]["out"].reshape(BATCH, SEQ, EMB)
```
